# Optimizing a Trainium2 kernel written in Bass

```python
import numpy as np
import jax
import jax.numpy as jnp

def _softmax(x, axis=-1):
    return jax.nn.softmax(x, axis=axis)

def _gelu(x):
    return jax.nn.gelu(x, approximate=True)

def _silu(x):
    return jax.nn.silu(x)

def _sigmoid(x):
    return jax.nn.sigmoid(x)

def _layernorm(x, axis=-1, eps=1e-05):
    m = jnp.mean(x, axis=axis, keepdims=True)
    v = jnp.var(x, axis=axis, keepdims=True)
    return (x - m) / jnp.sqrt(v + eps)

def _scatter_add(tgt, idx, src, axis=0):
    return tgt.at[idx].add(src)

def _segment_sum(src, seg, n):
    return jax.ops.segment_sum(src, seg, n)
kernel_name = 'mk_adj_resnorm_d4_adj_r2_2b5698'

def setup_inputs(seed: int=0):
    np.random.seed(seed)
    _w = jnp.asarray

    def _rec_inputs():
        import jax
        import jax.numpy as jnp
        _gk = jax.random.key(seed)
        x = -0.001547 + 1.001 * jax.random.normal(jax.random.fold_in(_gk, 1), (2048, 64), jnp.float32)
        _a = jax.random.bernoulli(jax.random.fold_in(_gk, 2), 0.00195312, (2048, 2048))
        _a = jnp.logical_or(_a, jnp.eye(2048, dtype=bool))
        _af = _a.astype(jnp.float32)
        _af = _af * jax.random.uniform(jax.random.fold_in(_gk, 3), (2048, 2048), jnp.float32, 0.05, 1)
        adj = _af
        return (x, adj)
    x, adj = _rec_inputs()

    def _L0_gnn_setup():
        import jax, jax.numpy as jnp
        import numpy as np

        def _laplacian(A):
            d = jnp.sum(A, axis=-1)
            dinv = 1.0 / jnp.sqrt(d)
            return A * dinv[:, None] * dinv[None, :]

        def _poly(A, theta):
            t = jax.nn.sigmoid(theta)
            N = A.shape[-1]
            P = jnp.eye(N, dtype=A.dtype)
            seg = P
            for i in range(theta.shape[0]):
                seg = seg @ A
                P = P + seg * t[i]
            return P
        key = jax.random.key(seed)
        k1, k2, k3, k4 = jax.random.split(key, 4)
        N, DIN, DOUT, K_CHEB = (2048, 64, 64, 2)
        return {'x': jax.random.normal(k1, (N, DIN), dtype=jnp.float32), 'A': jax.random.uniform(k2, (N, N), dtype=jnp.float32), 'theta': jax.random.normal(k3, (K_CHEB,), dtype=jnp.float32), 'W': jax.random.normal(k4, (DOUT, DIN), dtype=jnp.float32) / np.float32(np.sqrt(DIN)), 'b': jnp.zeros((DOUT,), dtype=jnp.float32), 'k': 4}
    _L0_gnn_all = _L0_gnn_setup()
    _L0_gnn_in = {k: v for k, v in _L0_gnn_all.items() if k in ('theta', 'W', 'b')}
    del _L0_gnn_all

    def _L1_gnn_setup():
        import jax, jax.numpy as jnp
        import numpy as np
        N = 5000
        DIM = 64
        F_CONST = 1.0
        B_CONST = 0.1
        R_CONST = 0.01
        key = jax.random.key(seed)
        k1, k2 = jax.random.split(key)
        t = jnp.zeros((1,), dtype=jnp.float32)
        x = jax.random.uniform(k1, (N, DIM), dtype=jnp.float32)
        A = jax.random.uniform(k2, (N, N), dtype=jnp.float32)
        return {'t': t, 'x': x, 'A': A}
    _L1_gnn_all = _L1_gnn_setup()
    _L1_gnn_in = {k: v for k, v in _L1_gnn_all.items() if k in ('t',)}
    del _L1_gnn_all

    def _L2_gnn_setup():
        import jax, jax.numpy as jnp
        import numpy as np
        N, D_IN, D_OUT = (8192, 64, 64)
        AVG_DEG = 32.0
        L2_EPS = 1e-12
        key = jax.random.key(seed)
        kx, ka, kw, kb = jax.random.split(key, 4)
        X = jax.random.normal(kx, (N, D_IN), dtype=jnp.float32)
        adj = (jax.random.uniform(ka, (N, N)) < AVG_DEG / N).astype(jnp.float32)
        bound = 1.0 / np.sqrt(2 * D_IN)
        W = jax.random.uniform(kw, (2 * D_IN, D_OUT), dtype=jnp.float32, minval=-bound, maxval=bound)
        b = jax.random.uniform(kb, (D_OUT,), dtype=jnp.float32, minval=-bound, maxval=bound)
        return {'X': X, 'adj': adj, 'W': W, 'b': b}
    _L2_gnn_all = _L2_gnn_setup()
    _L2_gnn_in = {k: v for k, v in _L2_gnn_all.items() if k in ('W', 'b')}
    del _L2_gnn_all

    def _L3_gnn_setup():
        import jax, jax.numpy as jnp
        import numpy as np
        N = 8192
        IN_C = 64
        OUT_C = 64
        key = jax.random.key(seed)
        k1, k2, k3 = jax.random.split(key, 3)
        x = jax.random.normal(k1, (N, IN_C), dtype=jnp.float32)
        adj = jax.random.uniform(k2, (N, N), dtype=jnp.float32)
        scale = jnp.sqrt(6.0 / (IN_C + OUT_C))
        weight = jax.random.uniform(k3, (IN_C, OUT_C), dtype=jnp.float32, minval=-scale, maxval=scale)
        return {'x': x, 'adj': adj, 'weight': weight}
    _L3_gnn_all = _L3_gnn_setup()
    _L3_gnn_in = {k: v for k, v in _L3_gnn_all.items() if k in ('weight',)}
    del _L3_gnn_all
    return {'x': x, 'adj': adj, 'L0_gnn_theta': _L0_gnn_in['theta'], 'L0_gnn_W': _L0_gnn_in['W'], 'L0_gnn_b': _L0_gnn_in['b'], 'L1_gnn_t': _L1_gnn_in['t'], 'L2_gnn_W': _L2_gnn_in['W'], 'L2_gnn_b': _L2_gnn_in['b'], 'L3_gnn_weight': _L3_gnn_in['weight']}

def reference(x, adj, L0_gnn_theta, L0_gnn_W, L0_gnn_b, L1_gnn_t, L2_gnn_W, L2_gnn_b, L3_gnn_weight):
    import jax
    import jax.numpy as jnp

    def _L0_gnn_ref(x, A, theta, W, b, k):
        import jax, jax.numpy as jnp
        import numpy as np

        def _laplacian(A):
            d = jnp.sum(A, axis=-1)
            dinv = 1.0 / jnp.sqrt(d)
            return A * dinv[:, None] * dinv[None, :]

        def _poly(A, theta):
            t = jax.nn.sigmoid(theta)
            N = A.shape[-1]
            P = jnp.eye(N, dtype=A.dtype)
            seg = P
            for i in range(theta.shape[0]):
                seg = seg @ A
                P = P + seg * t[i]
            return P
        S = _laplacian(A)
        S = _poly(S, theta)
        S = _laplacian(S)
        rank = jnp.argsort(jnp.argsort(-S, axis=-1), axis=-1)
        mask = jnp.where(rank < k, jnp.float32(1.0), jnp.float32(0.0))
        S = S * mask
        x = S @ x
        return x @ W.T + b

    def _L1_gnn_ref(t, x, A):
        import jax, jax.numpy as jnp
        import numpy as np
        N = 5000
        DIM = 64
        F_CONST = 1.0
        B_CONST = 0.1
        R_CONST = 0.01
        Ax = A @ x
        outer = R_CONST * jnp.sum(x * Ax, axis=1, keepdims=True)
        return F_CONST - B_CONST * x - outer

    def _L2_gnn_ref(X, adj, W, b):
        import jax, jax.numpy as jnp
        import numpy as np
        N, D_IN, D_OUT = (8192, 64, 64)
        AVG_DEG = 32.0
        L2_EPS = 1e-12
        deg = jnp.clip(jnp.sum(adj, axis=1, keepdims=True) + 1.0, 1.0, None)
        h_neigh = (adj @ X + X) / deg
        concat = jnp.concatenate([X, h_neigh], axis=1)
        z = concat @ W + b
        out = jax.nn.relu(z)
        norm = jnp.linalg.norm(out, axis=1, keepdims=True)
        return out / jnp.maximum(norm, L2_EPS)

    def _L3_gnn_ref(x, adj, weight):
        import jax, jax.numpy as jnp
        import numpy as np
        N = 8192
        IN_C = 64
        OUT_C = 64
        agg = adj @ x
        return agg @ weight
    x = _layernorm(x + _L0_gnn_ref(x, adj, L0_gnn_theta, L0_gnn_W, L0_gnn_b, 4), axis=-1)
    x = _layernorm(x + _L1_gnn_ref(L1_gnn_t, x, adj), axis=-1)
    x = _layernorm(x + _L2_gnn_ref(x, adj, L2_gnn_W, L2_gnn_b), axis=-1)
    x = _layernorm(x + _L3_gnn_ref(x, adj, L3_gnn_weight), axis=-1)
    return x

_drawn_inputs = setup_inputs


def setup_inputs(seed=0):
    import zlib

    import numpy as np

    out = dict(_drawn_inputs(seed))
    spreads = {'L0_gnn_b': (0.0, 0.1)}
    factors = {'L0_gnn_theta': 64.0, 'L2_gnn_b': 2.809}
    for name, (base, spread) in spreads.items():
        noise = np.random.default_rng([zlib.crc32(name.encode()), seed]).standard_normal(out[name].shape)
        drawn = base * np.exp(spread * noise) if base else spread * noise
        out[name] = jnp.asarray(drawn.astype(out[name].dtype))
    for name, factor in factors.items():
        out[name] = (out[name] * factor).astype(out[name].dtype)
    return out
```

```python
from contextlib import ExitStack

import concourse.bass as bass
from concourse import mybir


ALU = mybir.AluOpType
ACT = mybir.ActivationFunctionType
AX = mybir.AxisListType
F32 = mybir.dt.float32
F16 = mybir.dt.float16
U32 = mybir.dt.uint32

P = 128
A_SCALE = 2.0 ** 12
R_SCALE = 2.0 ** 14
V_SCALE = 2.0 ** 10
EPS = 1e-5
HI, LO = 0, 1


def wait_apart(eng, sem, value):
    if not isinstance(value, int):
        value = eng.to_reg(value)
        eng.wait_ge(sem, 1)
    eng.wait_ge(sem, value)


class Steps:

    def __init__(self, eng, sem):
        self.eng, self.sem, self.base, self.n = eng, sem, 0, 0

    def done(self, ins):
        ins.then_inc(self.sem, 1)
        self.n += 1

    def settle(self):
        self.eng.wait_ge(self.sem, self.base + self.n)

    def link(self, ins):
        self.done(ins)
        self.settle()

    def settle_apart(self):
        wait_apart(self.eng, self.sem, self.base + self.n)

    def link_apart(self, ins):
        self.done(ins)
        self.settle_apart()

    def enter(self, turn, per):
        self.start, self.per = self.base + self.n, per
        self.base, self.n = self.start + turn * per, 0

    def leave(self, turns):
        assert self.n == self.per, self.n
        self.base, self.n = self.start + turns * self.per, 0


def graph_layers(nc, xT, x, adj, theta, w0T, b0, w2, b2, w3, xw_dram, out):
    N, F = x.shape
    KB = N // P
    CW = 512
    CH = N // CW
    DIAG = CW // P
    TOP = 4
    SLOTS = KB + 4
    HELD = 6
    RELOADS = 4
    LAG = 3
    GB = 4
    NG = KB // GB

    with ExitStack() as ctx:
        def sb(name, shape, dt):
            return ctx.enter_context(nc.sbuf_tensor(name, shape, dt))

        def sem(name):
            return ctx.enter_context(nc.semaphore(name))

        at = sb("at", [P, 2, KB, N], F16)
        r_ring = sb("r_ring", [P, SLOTS, 2, CW], F16)
        rows = sb("rows", [P, 2, N], F32)
        nat = sb("nat", [P, 2, N], F16)
        xb = sb("xb", [P, KB, F], F32)
        cand = sb("cand", [P, 2, KB, CH * 8], F32)
        v_t = sb("v_t", [P, CW], F32)
        ident = sb("ident", [P, P], F32)
        ident16 = sb("ident16", [P, P], F16)
        ones = sb("ones", [P, P], F32)
        t0_diag = sb("t0_diag", [P, P], F32)
        w0_s = sb("w0_s", [F, F], F32)
        w2_s = sb("w2_s", [P, 2, 2 * F], F32)
        w3_s = sb("w3_s", [P, 2, F], F32)
        bias = sb("bias", [P, 2, F], F32)
        iota_u = sb("iota_u", [P, CH * 8], U32)
        iota_f = sb("iota_f", [P, CH * 8], F32)
        th = sb("th", [P, 2], F32)
        t01 = sb("t01", [P, 2], F32)
        t1_scaled = sb("t1_scaled", [P, 1], F32)
        t0_scaled = sb("t0_scaled", [P, 1], F32)
        d_scaled = sb("d_scaled", [P, KB], F32)
        c_row = sb("c_row", [P, KB], F32)
        dinv = sb("dinv", [P, KB], F32)
        droot = sb("droot", [P, KB], F32)
        vec = sb("vec", [P, KB], F32)
        vec16 = sb("vec16", [P, KB, 2], F16)
        mv_s = sb("mv_s", [P, KB, 2], F32)
        u_s = sb("u_s", [P, KB], F32)
        d2 = sb("d2", [P, KB], F32)
        dinv2 = sb("dinv2", [P, KB], F32)
        g_col = sb("g_col", [P, KB], F32)
        g_out = sb("g_out", [P, KB], F32)
        q_col = sb("q_col", [P, KB], F32)
        rdeg = sb("rdeg", [P, KB], F32)
        eps_s = sb("eps_s", [P, 1], F32)
        top8 = sb("top8", [P, 8], F32)
        pos8 = sb("pos8", [P, 8], U32)
        best = sb("best", [P, 2, 8], F32)
        best_pos = sb("best_pos", [P, 8], U32)
        best_posf = sb("best_posf", [P, TOP], F32)
        best_idx = sb("best_idx", [P, TOP], F32)
        gather_idx = sb("gather_idx", [P, 2, TOP], U32)
        stats = sb("stats", [P, GB, 6], F32)
        moments = sb("moments", [P, GB, 2], F32)
        sd = sb("sd", [P, GB], F32)
        rs = sb("rs", [P, GB], F32)
        red = sb("red", [P, GB], F32)

        banks = [ctx.enter_context(nc.psum_tensor(f"bank{i}", [P, 512], F32)) for i in range(8)]
        HELD_BANKS = [0, 1, 4, 5, 6, 7]
        TP = [banks[2], banks[3]]

        xT_s = r_ring[0:F, KB:SLOTS].rearrange("p a b c -> p (a b c)").bitcast(F32)
        xw_s = cand[:, :, :, :].rearrange("p a b c -> p (a b c)").rearrange("p (k f) -> p k f", f=F)
        g_bc = nat[:, :, :].rearrange("p a b -> p (a b)").bitcast(F32)
        reload = rows[:, 0, :].rearrange("p (s c) -> p s c", c=CW)
        gathered = reload[:, 0:1, :].rearrange("p a (u s f) -> p (a u) s f", u=2, f=F)
        prod = reload[:, 1, 0:TOP * F].rearrange("p (s f) -> p s f", f=F)
        h0 = reload[:, 1, TOP * F:TOP * F + F]
        y0 = reload[:, 1, TOP * F + F:TOP * F + 2 * F]
        onehot = reload[:, 2, 0:TOP * CH * 8].rearrange("p (s n) -> p s n", n=CH * 8)
        c_val = reload[:, 2, TOP * CH * 8:(TOP + 1) * CH * 8]
        c_idx = reload[:, 2, (TOP + 1) * CH * 8:(TOP + 2) * CH * 8]
        late = rows[:, 1, :]
        x1 = late[:, 0:KB * F].rearrange("p (k f) -> p k f", f=F)
        x1_pair = late[:, KB * F:2 * KB * F].bitcast(F16).rearrange("p (k u f) -> p k u f", u=2, f=F)

        end = r_ring[:, :, :, :].rearrange("p a b c -> p (a b c)").bitcast(F32)
        at_end = [0]

        def carve(width):
            at_end[0] += width
            return end[:, at_end[0] - width:at_end[0]]

        def carve_nodes():
            return carve(KB * F).rearrange("p (k f) -> p k f", f=F)

        x2, x3, u_top, u_bot = carve_nodes(), carve_nodes(), carve_nodes(), carve_nodes()
        pair2 = carve(KB * F).bitcast(F16).rearrange("p (k u f) -> p k u f", u=2, f=F)
        pair3 = carve(KB * F).bitcast(F16).rearrange("p (k u f) -> p k u f", u=2, f=F)
        ta = carve(GB * F).rearrange("p (k f) -> p k f", f=F)
        tb = carve(GB * F).rearrange("p (k f) -> p k f", f=F)
        tc = carve(GB * F).rearrange("p (k f) -> p k f", f=F)
        x_t = [carve(GB * F) for _ in range(2)]
        x4 = [carve(GB * F).rearrange("p (k f) -> p k f", f=F) for _ in range(2)]

        const_loaded = sem("const_loaded")
        xw_in_loaded = sem("xw_in_loaded")
        xb_loaded = sem("xb_loaded")
        rows_loaded = [sem("rows_loaded0"), sem("rows_loaded1")]
        reload_loaded = [sem(f"reload_loaded{i}") for i in range(RELOADS)]
        w_zeroed = sem("w_zeroed")
        xw_ready = sem("xw_ready")
        xw_copied = sem("xw_copied")
        xw_stored = sem("xw_stored")
        pool_step = sem("pool_step")
        ident_ready = sem("ident_ready")
        exp_done = sem("exp_done")
        t_ready = sem("t_ready")
        hi_ready = sem("hi_ready")
        lo_ready = sem("lo_ready")
        c_ready = sem("c_ready")
        rhi_ready = sem("rhi_ready")
        r_ready = sem("r_ready")
        r_used = sem("r_used")
        tp_ready = [sem("tp_ready0"), sem("tp_ready1")]
        tp_evac = [sem("tp_evac0"), sem("tp_evac1")]
        tile_ready = sem("tile_ready")
        tile_drained = sem("tile_drained")
        root_in = sem("root_in")
        root_out = sem("root_out")
        vec_ready = sem("vec_ready")
        mv_ready = sem("mv_ready")
        gdiag_ready = sem("gdiag_ready")
        gbank_ready = sem("gbank_ready")
        g_ready = sem("g_ready")
        idx_ready = sem("idx_ready")
        rows_gathered = [sem("rows_gathered0"), sem("rows_gathered1")]
        x1_ready = sem("x1_ready")
        acc_ready = sem("acc_ready")
        x_ready = sem("x_ready")
        xt_ready = sem("xt_ready")
        xt_copied = sem("xt_copied")
        u_ready = sem("u_ready")
        u_hi_ready = sem("u_hi_ready")
        u_read = sem("u_read")
        out_ready = sem("out_ready")
        out_stored = [sem("out_stored0"), sem("out_stored1")]
        dve_step = sem("dve_step")

        def a_block(part, k, i):
            return at[:, part, k, bass.ts(i, P)]

        def slot(c, k):
            return (KB * c + k) % SLOTS

        def bank_of(c, i):
            t = KB * c + i
            return banks[HELD_BANKS[t]] if t < HELD else banks[3] if t == HELD else banks[(i + 1) % 2]

        block = ctx.enter_context(nc.Block())

        @block.sync
        def _(sp):
            sp.dma_start(xT_s, xT).then_inc(xw_in_loaded, 16)
            sp.dma_start(w0_s[:, :], w0T).then_inc(xw_in_loaded, 16)
            sp.dma_start(th[:, :], theta.partition_broadcast(P)).then_inc(const_loaded, 16)
            for r in range(2):
                sp.dma_start(rows[:, r, :], adj[bass.ts(r, P), :]).then_inc(rows_loaded[r], 16)
            sp.dma_start(xb[:, :, :], x.rearrange("(k p) f -> p k f", p=P)).then_inc(xb_loaded, 16)
            sp.dma_start(bias[:, 0, :], b0.partition_broadcast(P)).then_inc(xb_loaded, 16)
            with sp.Fori(1, KB // 2) as pair:
                for u in range(2):
                    sp.wait_ge(r_ready, pair * 2 + (u - 1))
                    sp.dma_start(rows[:, u, :], adj[bass.ds((pair * 2 + u) * P, P), :]).then_inc(rows_loaded[u], 16)
            sp.wait_ge(xw_copied, 2)
            sp.dma_start(xw_dram.rearrange("(k p) f -> p k f", p=P), xw_s).then_inc(xw_stored, 16)
            sp.dma_start(bias[:, 1, :], b2.partition_broadcast(P)).then_inc(const_loaded, 16)
            sp.wait_ge(w_zeroed, 2)
            for half in range(2):
                sp.dma_start(w2_s[half * F:half * F + F, half, :], w2).then_inc(const_loaded, 16)
                sp.dma_start(w3_s[half * F:half * F + F, half, :], w3).then_inc(const_loaded, 16)
            sp.wait_ge(r_ready, KB)
            for n in range(KB, CH * KB):
                c, k = n // KB, n % KB
                if n - KB >= RELOADS:
                    sp.wait_ge(r_ready, n - RELOADS + 1)
                sp.dma_start(reload[:, n % RELOADS, :], adj[bass.ts(k, P), bass.ts(c, CW)]) \
                    .then_inc(reload_loaded[n % RELOADS], 16)
            out_v = out.rearrange("(k p) f -> p k f", p=P)
            for g in range(NG):
                sp.wait_ge(out_ready, g + 1)
                sp.dma_start(out_v[:, g * GB:g * GB + GB, :], x4[g % 2]).then_inc(out_stored[g % 2], 16)
            for u in range(2):
                sp.wait_ge(out_stored[u], 16 * NG // 2)

        @block.gpsimd
        def _(pool):
            nc.gpsimd.memset(ones[:, :], 1.0).then_inc(pool_step, 1)
            pool.wait_ge(pool_step, 1)
            nc.gpsimd.affine_select(out=ident[:, :], in_=ones[:, :], compare_op=ALU.is_equal, fill=0.0, base=0,
                                    pattern=[[-1, P]], channel_multiplier=1).then_inc(pool_step, 1)
            pool.wait_ge(pool_step, 2)
            nc.gpsimd.tensor_copy(ident16[:, :], ident[:, :]).then_inc(ident_ready, 1)
            nc.gpsimd.iota(iota_u[:, :], pattern=[[1, CH * 8]], base=0, channel_multiplier=0).then_inc(pool_step, 1)
            pool.wait_ge(pool_step, 3)
            nc.gpsimd.tensor_copy(iota_f[:, :], iota_u[:, :]).then_inc(ident_ready, 1)

            nc.gpsimd.memset(w2_s[:, :, :], 0.0).then_inc(w_zeroed, 1)
            nc.gpsimd.memset(w3_s[:, :, :], 0.0).then_inc(w_zeroed, 1)

            def gather(i, u):
                wait_apart(pool, idx_ready, i + 1)
                for s in range(TOP):
                    pool.indirect_dma_start(
                        out=gathered[:, u, s, :], out_offset=None, in_=xw_dram,
                        in_offset=bass.IndirectOffsetOnAxis(ap=gather_idx[:, u, s:s + 1], axis=0),
                    ).then_inc(rows_gathered[u], 16)

            pool.wait_ge(xw_stored, 16)
            with pool.Fori(0, KB // 2) as pair:
                gather(pair * 2, 0)
                gather(pair * 2 + 1, 1)

        @block.scalar
        def _(act):
            act.wait_ge(const_loaded, 16)
            nc.scalar.activation(t01[:, :], th[:, :], ACT.Exp, scale=-1.0).then_inc(exp_done, 1)
            for h in range(2):
                act.wait_ge(xw_ready, h + 1)
                nc.scalar.copy(xw_s[:, h * KB // 2:(h + 1) * KB // 2, :],
                               TP[h][:, :].rearrange("p (k f) -> p k f", f=F)).then_inc(xw_copied, 1)

            def split_hi(r, u, turn):
                act.wait_ge(rows_loaded[u], 16 * turn + 16)
                if isinstance(r, int) and r == 0:
                    pass
                else:
                    act.wait_ge(tp_ready[1], 2 * r - 1)
                nc.scalar.activation(nat[:, HI, :], rows[:, u, :], ACT.Copy, scale=A_SCALE,
                                     accum_out=d_scaled[:, bass.ds(r, 1)]).then_inc(hi_ready, 1)

            def evacuate(r, part):
                act.wait_ge(tp_ready[0], 2 * r + part + 1)
                nc.scalar.copy(at[:, part, 0:KB // 2, bass.ds(r * P, P)],
                               TP[0][:, :].bitcast(F16).rearrange("p (k c) -> p k c", c=P)).then_inc(tp_evac[0], 1)

            def row_block(r, u, turn, following=True):
                evacuate(r, HI)
                act.wait_ge(c_ready, r + 1)
                nc.scalar.activation(r_ring[:, bass.ds(r, 1), HI, :].rearrange("p a c -> p (a c)"),
                                     rows[:, u, 0:CW], ACT.Copy, scale=c_row[:, bass.ds(r, 1)]).then_inc(rhi_ready, 1)
                if following:
                    split_hi(r + 1, 1 - u, turn + u)
                evacuate(r, LO)

            split_hi(0, 0, 0)
            for r in range(4):
                row_block(r, r % 2, r // 2)
            with act.Fori(2, KB // 2 - 1) as pair:
                row_block(pair * 2, 0, pair)
                row_block(pair * 2 + 1, 1, pair)
            row_block(KB - 2, 0, KB // 2 - 1)
            row_block(KB - 1, 1, KB // 2 - 1, following=False)

            act.wait_ge(root_in, 1)
            nc.scalar.activation(droot[:, :], u_s[:, :], ACT.Sqrt).then_inc(root_out, 1)
            act.wait_ge(root_in, 2)
            nc.scalar.activation(dinv2[:, :], d2[:, :], ACT.Sqrt).then_inc(root_out, 1)
            for q in range(CH):
                act.wait_ge(gbank_ready, q + 1)
                nc.scalar.copy(g_bc[:, bass.ts(q, CW)], banks[2][:, :]).then_inc(g_ready, 1)

            for n in range(KB, CH * KB):
                c, k = n // KB, n % KB
                act.wait_ge(reload_loaded[n % RELOADS], 16 * ((n - KB) // RELOADS + 1))
                if k >= SLOTS - KB:
                    act.wait_ge(r_used, (KB - 1) * (c - 1) + k - (SLOTS - KB) + 1)
                elif c >= 2:
                    act.wait_ge(tile_ready, KB * (c - 1))
                else:
                    act.wait_ge(xw_ready, 2)
                nc.scalar.activation(r_ring[:, slot(c, k), HI, :], reload[:, n % RELOADS, :], ACT.Copy,
                                     scale=c_row[:, k:k + 1]).then_inc(rhi_ready, 1)

            roots = [2]

            def root(out_ap, in_ap, bias_ap=0.0):
                roots[0] += 1
                act.wait_ge(root_in, roots[0])
                nc.scalar.activation(out_ap, in_ap, ACT.Sqrt, bias=bias_ap).then_inc(root_out, 1)

            with act.Fori(0, KB) as i:
                act.wait_ge(root_in, i + 3)
                nc.scalar.activation(sd[:, 0:1], moments[:, 0, 1:2], ACT.Sqrt, bias=eps_s[:, 0:1]).then_inc(root_out, 1)
            roots[0] += KB
            for g in range(NG):
                root(sd[:, :], moments[:, :, 1], eps_s[:, 0:1])

            def feature_halves(n, pair, width):
                g = n % NG
                act.wait_ge(xt_ready, n + 1)
                nc.scalar.copy(x_t[n % 2], banks[2 * (n % 2)][:, 0:GB * F]).then_inc(xt_copied, 1)
                act.wait_ge(u_ready, n + 1)
                u = banks[2 * (n % 2) + 1][:, 0:GB * width].rearrange("p (k f) -> p k f", f=width)
                nc.scalar.activation(pair[:, g * GB:g * GB + GB, HI, :], u[:, :, width - F:width], ACT.Copy,
                                     scale=V_SCALE).then_inc(u_hi_ready, 1)

            for g in range(NG):
                feature_halves(g, pair2, 2 * F)
            for g in range(NG):
                root(red[:, :], sd[:, :])
                root(sd[:, :], moments[:, :, 1], eps_s[:, 0:1])
            for g in range(NG):
                feature_halves(NG + g, pair3, F)
            for g in range(NG):
                root(sd[:, :], moments[:, :, 1], eps_s[:, 0:1])

        @block.vector
        def _(dve):
            step = Steps(dve, dve_step)
            link = step.link
            roots = [0]

            def nat_lo(r, u):
                dve.wait_ge(hi_ready, r + 1)
                if not (isinstance(r, int) and r == 0):
                    dve.wait_ge(tp_ready[1], 2 * r)
                nc.vector.scalar_tensor_tensor(nat[:, LO, :], rows[:, u, :], A_SCALE, nat[:, HI, :],
                                               ALU.mult, ALU.subtract).then_inc(lo_ready, 1)

            def row_scale(r):
                link(nc.vector.reciprocal(c_row[:, bass.ds(r, 1)], d_scaled[:, bass.ds(r, 1)]))
                nc.vector.tensor_scalar(c_row[:, bass.ds(r, 1)], c_row[:, bass.ds(r, 1)], t1_scaled[:, 0:1], None,
                                        ALU.mult).then_inc(c_ready, 1)

            def r_lo(dst, src, scale, n, diag):
                dve.wait_ge(rhi_ready, n + 1)
                if diag is None:
                    nc.vector.scalar_tensor_tensor(dst[:, LO, :], src, scale, dst[:, HI, :],
                                                   ALU.mult, ALU.subtract).then_inc(r_ready, 1)
                    return
                link(nc.vector.scalar_tensor_tensor(dst[:, LO, :], src, scale, dst[:, HI, :],
                                                    ALU.mult, ALU.subtract))
                cols = slice(diag * P, diag * P + P)
                link(nc.vector.scalar_tensor_tensor(v_t[:, 0:P], src[:, cols], scale, t0_diag[:, :],
                                                    ALU.mult, ALU.add))
                link(nc.vector.tensor_copy(dst[:, HI, cols], v_t[:, 0:P]))
                nc.vector.tensor_tensor(dst[:, LO, cols], v_t[:, 0:P], dst[:, HI, cols],
                                        ALU.subtract).then_inc(r_ready, 1)
                dve.wait_ge(r_ready, n + 1)

            def evacuate(r, part):
                dve.wait_ge(tp_ready[1], 2 * r + part + 1)
                nc.vector.tensor_copy(at[:, part, KB // 2:KB, bass.ds(r * P, P)],
                                      TP[1][:, :].bitcast(F16).rearrange("p (k c) -> p k c", c=P)) \
                    .then_inc(tp_evac[1], 1)

            def row_block(r, u):
                nat_lo(r, u)
                row_scale(r)
                evacuate(r, HI)
                dve.wait_ge(c_ready, r + 1)
                r_lo(r_ring[:, bass.ds(r, 1)].rearrange("p a b c -> p (a b) c"), rows[:, u, 0:CW],
                     c_row[:, bass.ds(r, 1)], r, r if isinstance(r, int) and r < DIAG else None)
                evacuate(r, LO)

            nc.vector.memset(eps_s[:, :], EPS)
            dve.wait_ge(exp_done, 1)
            link(nc.vector.tensor_scalar(t01[:, :], t01[:, :], 1.0, None, ALU.add))
            link(nc.vector.reciprocal(t01[:, :], t01[:, :]))
            link(nc.vector.tensor_scalar(t1_scaled[:, :], t01[:, 1:2], A_SCALE * R_SCALE, None, ALU.mult))
            link(nc.vector.tensor_scalar(t0_scaled[:, :], t01[:, 0:1], R_SCALE, None, ALU.mult))
            dve.wait_ge(ident_ready, 2)
            link(nc.vector.tensor_scalar(t0_diag[:, :], ident[:, :], t0_scaled[:, 0:1], None, ALU.mult))

            for r in range(4):
                row_block(r, r % 2)
            with dve.Fori(2, KB // 2) as pair:
                step.enter(pair - 2, 2)
                row_block(pair * 2, 0)
                row_block(pair * 2 + 1, 1)
                step.leave(KB // 2 - 2)

            def root(value):
                value.then_inc(root_in, 1)
                roots[0] += 1

            def wait_root():
                dve.wait_ge(root_out, roots[0])

            def split_vec():
                link(nc.vector.tensor_scalar(vec[:, :], vec[:, :], V_SCALE, None, ALU.mult))
                link(nc.vector.tensor_copy(vec16[:, :, HI], vec[:, :]))
                nc.vector.tensor_tensor(vec16[:, :, LO], vec[:, :], vec16[:, :, HI], ALU.subtract) \
                    .then_inc(vec_ready, 1)

            def matvec_out(n):
                dve.wait_ge(mv_ready, n + 1)
                link(nc.vector.tensor_copy(mv_s[:, :, :], banks[2][:, 0:2 * KB].rearrange("p (k t) -> p k t", t=2)))
                link(nc.vector.tensor_tensor(vec[:, :], mv_s[:, :, 0], mv_s[:, :, 1], ALU.add))
                link(nc.vector.tensor_scalar(vec[:, :], vec[:, :], 1.0 / (A_SCALE * V_SCALE), None, ALU.mult))

            root(nc.vector.tensor_scalar(u_s[:, :], d_scaled[:, :], 1.0 / A_SCALE, None, ALU.mult))
            dve.wait_ge(root_in, 1)
            link(nc.vector.tensor_scalar(rdeg[:, :], u_s[:, :], 1.0, 1.0, ALU.add, ALU.max))
            link(nc.vector.reciprocal(rdeg[:, :], rdeg[:, :]))
            wait_root()
            link(nc.vector.reciprocal(dinv[:, :], droot[:, :]))
            link(nc.vector.tensor_copy(vec[:, :], dinv[:, :]))
            split_vec()
            matvec_out(0)
            link(nc.vector.tensor_tensor(u_s[:, :], vec[:, :], dinv[:, :], ALU.mult))
            link(nc.vector.tensor_tensor(vec[:, :], u_s[:, :], dinv[:, :], ALU.mult))
            split_vec()
            matvec_out(1)
            link(nc.vector.tensor_tensor(vec[:, :], vec[:, :], dinv[:, :], ALU.mult))
            link(nc.vector.tensor_scalar(d2[:, :], u_s[:, :], t01[:, 0:1], 1.0, ALU.mult, ALU.add))
            root(nc.vector.scalar_tensor_tensor(d2[:, :], vec[:, :], t01[:, 1:2], d2[:, :], ALU.mult, ALU.add))
            wait_root()
            link(nc.vector.reciprocal(dinv2[:, :], dinv2[:, :]))
            link(nc.vector.tensor_tensor(g_col[:, :], dinv[:, :], dinv2[:, :], ALU.mult))
            step.done(nc.vector.tensor_scalar(g_out[:, :], g_col[:, :], 1.0 / (A_SCALE * R_SCALE), None, ALU.mult))
            link(nc.vector.scalar_tensor_tensor(q_col[:, :], dinv2[:, :], A_SCALE * R_SCALE, droot[:, :],
                                                ALU.mult, ALU.mult))
            for q in range(CH):
                if q:
                    dve.wait_ge(gbank_ready, q)
                nc.vector.tensor_tensor(v_t[:, :].rearrange("p (k c) -> p k c", c=P),
                                        ident[:, :].unsqueeze(1).to_broadcast([P, DIAG, P]),
                                        g_col[:, q * DIAG:q * DIAG + DIAG].unsqueeze(2).to_broadcast([P, DIAG, P]),
                                        ALU.mult).then_inc(gdiag_ready, 1)
            dve.wait_ge(gbank_ready, CH)
            dve.wait_ge(g_ready, CH)
            dve.wait_ge(xb_loaded, 32)
            link(nc.vector.tensor_tensor(xb[:, :, :], xb[:, :, :],
                                         bias[:, 0, :].unsqueeze(1).to_broadcast([P, KB, F]), ALU.add))
            dve.wait_ge(xw_stored, 16)

            def drain(c, i, bank, diag):
                dve.wait_ge(tile_ready, i + (KB * c + 1))
                nc.vector.tensor_tensor(v_t[:, :], bank[:, :], g_bc[:, bass.ts(c, CW)], ALU.mult) \
                    .then_inc(tile_drained, 1)
                wait_apart(dve, tile_drained, i + (KB * c + 1))
                if diag:
                    cols = slice((i % DIAG) * P, (i % DIAG) * P + P)
                    link(nc.vector.scalar_tensor_tensor(v_t[:, cols], ident[:, :], q_col[:, i:i + 1], v_t[:, cols],
                                                        ALU.mult, ALU.add))
                if c < CH - 1:
                    step.link_apart(nc.vector.max(top8[:, :], v_t[:, :]))
                    step.done(nc.vector.max_index(pos8[:, :], top8[:, :], v_t[:, :]))
                    step.done(nc.vector.tensor_copy(cand[:, 0, bass.ds(i, 1), c * 8:c * 8 + 8].squeeze(1), top8[:, :]))
                    step.settle()
                    link(nc.vector.tensor_scalar(cand[:, 1, bass.ds(i, 1), c * 8:c * 8 + 8].squeeze(1), pos8[:, :],
                                                 float(c * CW), None, ALU.add))

            def next_r(c, k):
                n = KB * (c + 1) + k
                r_lo(r_ring[:, slot(c + 1, k)], reload[:, n % RELOADS, :], c_row[:, k:k + 1], n,
                     k - (c + 1) * DIAG if k // DIAG == c + 1 else None)

            EARLY = SLOTS - KB
            for c in range(CH - 1):
                def drains(a, b):
                    i = a
                    while i < b:
                        if i // DIAG == c or KB * c + i < HELD + 2 or i % 2 or i + 1 >= b:
                            drain(c, i, bank_of(c, i), i // DIAG == c)
                            i += 1
                            continue
                        to = i
                        while to + 2 <= b and to // DIAG != c:
                            to += 2
                        with dve.Fori(i // 2, to // 2) as pair:
                            step.enter(pair - i // 2, 8)
                            drain(c, pair * 2, bank_of(c, i), False)
                            drain(c, pair * 2 + 1, bank_of(c, i + 1), False)
                            step.leave((to - i) // 2)
                        i = to

                drains(0, 8)
                for k in range(EARLY):
                    next_r(c, k)
                drains(8, KB - 1)
                for k in range(EARLY, KB):
                    next_r(c, k)
                drain(c, KB - 1, bank_of(c, KB - 1), (KB - 1) // DIAG == c)

            def normalise(out_aps, h, count):
                for b in range(count):
                    step.done(nc.vector.bn_stats(stats[:, b, :], h[b]))
                step.settle_apart()
                for b in range(count):
                    ins = nc.vector.bn_aggr(moments[:, b, :], stats[:, b, :])
                    if b < count - 1:
                        step.done(ins)
                return ins

            def select(i, u, diag):
                c = CH - 1
                last = slice(c * 8, c * 8 + 8)
                drain(c, i, bank_of(c, u), diag)
                step.done(nc.vector.tensor_copy(c_val[:, 0:c * 8], cand[:, 0, bass.ds(i, 1), 0:c * 8].squeeze(1)))
                step.done(nc.vector.tensor_copy(c_idx[:, 0:c * 8], cand[:, 1, bass.ds(i, 1), 0:c * 8].squeeze(1)))
                step.link_apart(nc.vector.max(c_val[:, last], v_t[:, :]))
                link(nc.vector.max_index(pos8[:, :], c_val[:, last], v_t[:, :]))
                step.link_apart(nc.vector.tensor_scalar(c_idx[:, last], pos8[:, :], float(c * CW), None, ALU.add))
                step.link_apart(nc.vector.max(best[:, u, :], c_val))
                link(nc.vector.max_index(best_pos[:, :], best[:, u, :], c_val))
                link(nc.vector.tensor_copy(best_posf[:, :], best_pos[:, 0:TOP]))
                link(nc.vector.tensor_tensor(onehot[:, :, :], iota_f[:, :].unsqueeze(1).to_broadcast([P, TOP, CH * 8]),
                                             best_posf[:, :].unsqueeze(2).to_broadcast([P, TOP, CH * 8]),
                                             ALU.is_equal))
                link(nc.vector.tensor_tensor(onehot[:, :, :], onehot[:, :, :],
                                             c_idx.unsqueeze(1).to_broadcast([P, TOP, CH * 8]), ALU.mult))
                link(nc.vector.tensor_reduce(best_idx[:, :], onehot[:, :, :], AX.X, ALU.add))
                nc.vector.tensor_copy(gather_idx[:, u, :], best_idx[:, :]).then_inc(idx_ready, 1)

            def finish(i, u, turn):
                dve.wait_ge(rows_gathered[u], 64 * turn + 64)
                link(nc.vector.tensor_tensor(prod, gathered[:, u, :, :],
                                             best[:, u, 0:TOP].unsqueeze(2).to_broadcast([P, TOP, F]), ALU.mult))
                link(nc.vector.tensor_reduce(y0, prod.rearrange("p s f -> p f s"), AX.X, ALU.add))
                link(nc.vector.scalar_tensor_tensor(h0, y0, g_out[:, bass.ds(i, 1)],
                                                    xb[:, bass.ds(i, 1), :].squeeze(1), ALU.mult, ALU.add))
                normalise(None, [h0], 1).then_inc(root_in, 1)
                dve.wait_ge(root_out, i + 3)
                link(nc.vector.reciprocal(rs[:, 0:1], sd[:, 0:1]))
                link(nc.vector.tensor_scalar(x1[:, bass.ds(i, 1), :].squeeze(1), h0, moments[:, 0, 0:1], rs[:, 0:1],
                                             ALU.subtract, ALU.mult))
                link(nc.vector.tensor_scalar(x1_pair[:, bass.ds(i, 1), HI, :].squeeze(1),
                                             x1[:, bass.ds(i, 1), :].squeeze(1), V_SCALE, None, ALU.mult))
                nc.vector.scalar_tensor_tensor(x1_pair[:, bass.ds(i, 1), LO, :].squeeze(1),
                                               x1[:, bass.ds(i, 1), :].squeeze(1), V_SCALE,
                                               x1_pair[:, bass.ds(i, 1), HI, :].squeeze(1),
                                               ALU.mult, ALU.subtract).then_inc(x1_ready, 1)

            FIN = 7
            SEL = 11
            first_diag = (CH - 1) * DIAG
            dve.wait_ge(r_ready, CH * KB)
            select(0, 0, False)
            with dve.Fori(0, first_diag // 2 - 1) as pair:
                step.enter(pair, 2 * (SEL + FIN))
                select(pair * 2 + 1, 1, False)
                finish(pair * 2, 0, pair)
                select(pair * 2 + 2, 0, False)
                finish(pair * 2 + 1, 1, pair)
                step.leave(first_diag // 2 - 1)
            for i in range(first_diag - 1, KB):
                select(i, i % 2, i >= first_diag)
                finish(i - 1, (i - 1) % 2, (i - 1) // 2)
            finish(KB - 1, 1, (KB - 1) // 2)
            roots[0] += KB

            def group(t, g):
                return t[:, g * GB:g * GB + GB, :]

            def spread(col):
                return col.unsqueeze(2).to_broadcast([P, GB, F])

            def norm_group(dst, h, signal, count):
                root(normalise(None, [h[:, b, :] for b in range(GB)], GB))
                wait_root()
                link(nc.vector.reciprocal(rs[:, :], sd[:, :]))
                for b in range(GB):
                    ins = nc.vector.tensor_scalar(dst[:, b, :], h[:, b, :], moments[:, b, 0:1], rs[:, b:b + 1],
                                                  ALU.subtract, ALU.mult)
                    if b < GB - 1:
                        step.done(ins)
                ins.then_inc(signal, 1)
                dve.wait_ge(signal, count)

            unscale = 1.0 / (A_SCALE * V_SCALE)

            def acc(layer, g):
                return banks[[4, 6, 4][layer] + g * GB * F // 512][:, (g * GB * F) % 512:(g * GB * F) % 512 + GB * F] \
                    .rearrange("p (k f) -> p k f", f=F)

            for g in range(NG):
                link(nc.vector.tensor_scalar(tb, group(x1, g), -0.1, 1.0, ALU.mult, ALU.add))
                link(nc.vector.tensor_tensor(tb, tb, group(x1, g), ALU.add))
                dve.wait_ge(acc_ready, 1)
                link(nc.vector.scalar_tensor_tensor(ta, acc(0, g), unscale, group(x1, g), ALU.mult, ALU.mult))
                link(nc.vector.tensor_reduce(red[:, :], ta, AX.X, ALU.add))
                link(nc.vector.scalar_tensor_tensor(ta, spread(red[:, :]), -0.01, tb, ALU.mult, ALU.add))
                norm_group(group(x2, g), ta, x_ready, g + 1)

            dve.wait_ge(const_loaded, 96)

            def feature_lo(n, pair, width):
                g = n % NG
                dve.wait_ge(u_hi_ready, n + 1)
                u = banks[2 * (n % 2) + 1][:, 0:GB * width].rearrange("p (k f) -> p k f", f=width)
                step.done(nc.vector.scalar_tensor_tensor(group(pair[:, :, LO, :], g), u[:, :, width - F:width],
                                                         V_SCALE, group(pair[:, :, HI, :], g),
                                                         ALU.mult, ALU.subtract))
                if width == 2 * F:
                    step.done(nc.vector.tensor_copy(group(u_bot, g), u[:, :, F:2 * F]))
                    step.done(nc.vector.tensor_tensor(group(u_top, g), u[:, :, 0:F],
                                                      bias[:, 1, :].unsqueeze(1).to_broadcast([P, GB, F]), ALU.add))
                step.settle()
                nc.vector.tensor_copy(rs[:, 0:1], eps_s[:, 0:1]).then_inc(u_read, 1)
                dve.wait_ge(u_read, n + 1)

            for g in range(NG):
                feature_lo(g, pair2, 2 * F)
            for g in range(NG):
                dve.wait_ge(acc_ready, 2)
                link(nc.vector.scalar_tensor_tensor(ta, acc(1, g), unscale, group(u_bot, g), ALU.mult, ALU.add))
                link(nc.vector.tensor_tensor(ta, ta, spread(rdeg[:, g * GB:g * GB + GB]), ALU.mult))
                link(nc.vector.tensor_tensor(ta, ta, group(u_top, g), ALU.add))
                link(nc.vector.tensor_scalar(ta, ta, 0.0, None, ALU.max))
                link(nc.vector.tensor_tensor(tb, ta, ta, ALU.mult))
                root(nc.vector.tensor_reduce(sd[:, :], tb, AX.X, ALU.add))
                wait_root()
                link(nc.vector.tensor_scalar(red[:, :], red[:, :], 1e-12, None, ALU.max))
                link(nc.vector.reciprocal(red[:, :], red[:, :]))
                link(nc.vector.tensor_tensor(tb, ta, spread(red[:, :]), ALU.mult))
                link(nc.vector.tensor_tensor(tc, tb, group(x2, g), ALU.add))
                norm_group(group(x3, g), tc, x_ready, NG + g + 1)

            for g in range(NG):
                feature_lo(NG + g, pair3, F)
            for g in range(NG):
                dve.wait_ge(acc_ready, 3)
                link(nc.vector.scalar_tensor_tensor(ta, acc(2, g), unscale, group(x3, g), ALU.mult, ALU.add))
                if g >= 2:
                    dve.wait_ge(out_stored[g % 2], 16 * (g // 2))
                norm_group(x4[g % 2], ta, out_ready, g + 1)

        @block.tensor
        def _(pe):
            pe.wait_ge(xw_in_loaded, 32)
            for k in range(KB):
                ins = nc.tensor.matmul(TP[k // (KB // 2)][:, bass.ts(k % (KB // 2), F)], xT_s[:, bass.ts(k, P)],
                                       w0_s[:, :], start=True, stop=True)
                if k % (KB // 2) == KB // 2 - 1:
                    ins.then_inc(xw_ready, 1)

            def transposes(r, part):
                pe.wait_ge([hi_ready, lo_ready][part], r + 1)
                for h in range(2):
                    if isinstance(r, int) and r == 0 and part == 0:
                        pe.wait_ge(xw_copied, h + 1)
                    else:
                        pe.wait_ge(tp_evac[h], 2 * r + part)
                    for k in range(KB // 2):
                        ins = nc.tensor.transpose(TP[h][:, :].bitcast(F16)[:, bass.ts(k, P)],
                                                  nat[:, part, bass.ts(h * KB // 2 + k, P)], ident16[:, :])
                    ins.then_inc(tp_ready[h], 1)

            def triple(acc, rhs_hi, rhs_lo, k, i, start, stop, skip=False):
                nc.tensor.matmul(acc, a_block(HI, k, i), rhs_hi, start=start, stop=False, skip_group_check=skip)
                nc.tensor.matmul(acc, a_block(HI, k, i), rhs_lo, start=False, stop=False, skip_group_check=skip)
                return nc.tensor.matmul(acc, a_block(LO, k, i), rhs_hi, start=False, stop=stop,
                                        skip_group_check=skip)

            def r_block(s, part):
                return r_ring[:, s, part, :] if isinstance(s, int) \
                    else r_ring[:, bass.ds(s, 1), part, :].squeeze(1)

            def held_step(s, tiles, last=False):
                for h in range(2):
                    pe.wait_ge(tp_evac[h], 2 * s + 2)
                pe.wait_ge(r_ready, s + 1)
                for i in range(tiles):
                    first = isinstance(s, int) and i == s
                    for k in (range(s + 1) if first else [s]):
                        ins = triple(banks[HELD_BANKS[i]][:, :], r_block(k, HI), r_block(k, LO), k, i,
                                     first and k == 0, last)
                    if last:
                        ins.then_inc(tile_ready, 1)

            pe.wait_ge(ident_ready, 1)
            transposes(0, HI)
            transposes(0, LO)
            for r in range(1, HELD + 1):
                transposes(r, HI)
                held_step(r - 1, min(r, HELD))
                transposes(r, LO)
            with pe.Fori(HELD + 1, KB) as r:
                transposes(r, HI)
                held_step(r - 1, HELD)
                transposes(r, LO)
            held_step(KB - 1, HELD, last=True)

            def matvec(n):
                pe.wait_ge(vec_ready, n + 1)
                with pe.Fori(0, KB) as i:
                    for k in range(KB):
                        nc.tensor.matmul(banks[2][:, bass.ds(i * 2, 2)], a_block(HI, k, i), vec16[:, k, :],
                                         start=(k == 0), stop=False, skip_group_check=True)
                        nc.tensor.matmul(banks[2][:, bass.ds(i * 2, 1)], a_block(LO, k, i), vec16[:, k, HI:HI + 1],
                                         start=False, stop=(k == KB - 1), skip_group_check=True)
                nc.tensor.matmul(banks[2][:, 2 * KB:2 * KB + 1], ident16[:, :], ident16[:, 0:1],
                                 start=True, stop=True).then_inc(mv_ready, 1)

            def tile(c, i, bank, first=False, last=False):
                if KB * c + (i if isinstance(i, int) else HELD + 2) > HELD:
                    before = 0 if c == 0 and isinstance(i, int) and i == HELD + 1 else \
                        1 if c == 0 and isinstance(i, int) and i == HELD + 2 else None
                    pe.wait_ge(tile_drained, i + (KB * c - 1) if before is None else before + 1)
                for k in range(KB):
                    if first:
                        pe.wait_ge(r_ready, KB * c + k + 1)
                    s = slot(c, k)
                    ins = triple(bank[:, :], r_ring[:, s, HI, :], r_ring[:, s, LO, :], k, i, k == 0, k == KB - 1)
                    if last and k < KB - 1:
                        ins.then_inc(r_used, 1)
                ins.then_inc(tile_ready, 1)

            for h in range(2):
                pe.wait_ge(tp_evac[h], 2 * KB)
            matvec(0)
            tile(0, HELD, banks[3])
            matvec(1)
            for q in range(CH):
                pe.wait_ge(gdiag_ready, q + 1)
                if q:
                    pe.wait_ge(g_ready, q)
                nc.tensor.matmul(banks[2][:, :], ones[:, :], v_t[:, :], start=True, stop=True) \
                    .then_inc(gbank_ready, 1)

            def tiles(c, a, b):
                with pe.Fori(a // 2, b // 2) as pair:
                    tile(c, pair * 2, bank_of(c, a))
                    tile(c, pair * 2 + 1, bank_of(c, a + 1))

            for c in range(CH - 1):
                a = HELD + 1 if c == 0 else 0
                tile(c, a, bank_of(c, a), first=(c > 0))
                a += 1
                if a % 2 or c == 0:
                    tile(c, a, bank_of(c, a))
                    a += 1
                if a % 2:
                    tile(c, a, bank_of(c, a))
                    a += 1
                tiles(c, a, KB - 2)
                tile(c, KB - 2, bank_of(c, KB - 2))
                tile(c, KB - 1, bank_of(c, KB - 1), last=True)

            def aggregate(first_bank, pair, k):
                per = 512 // F
                edge = isinstance(k, int)
                for i in range(KB):
                    rhs = [pair[:, k, u, :] if edge else pair[:, bass.ds(k, 1), u, :].squeeze(1) for u in range(2)]
                    ins = triple(banks[first_bank + i // per][:, bass.ts(i % per, F)], rhs[HI], rhs[LO], k, i,
                                 edge and k == 0 and i % per == 0, edge and k == KB - 1, skip=True)
                return ins

            def layer1(k):
                pe.wait_ge(x1_ready, k + 1)
                return aggregate(4, x1_pair, k)

            c = CH - 1
            for i in range(LAG + 1):
                tile(c, i, bank_of(c, i), first=(i == 0))
            layer1(0)
            with pe.Fori((LAG + 1) // 2, KB // 2 - 1) as pair:
                for u in range(2):
                    tile(c, pair * 2 + u, bank_of(c, u))
                    layer1(pair * 2 + (u - LAG))
            for i in range(KB - 2, KB):
                tile(c, i, bank_of(c, i))
                layer1(i - LAG)
            for k in range(KB - LAG, KB - 1):
                layer1(k)
            layer1(KB - 1).then_inc(acc_ready, 1)

            def project(n, w, width):
                g = n % NG
                src = [x2, x3][n // NG]
                pe.wait_ge(x_ready, n + 1)
                if n >= 2:
                    pe.wait_ge(u_read, n - 1)
                for b in range(0, GB, 2):
                    ins = nc.tensor.transpose(banks[2 * (n % 2)][:, bass.ts(b // 2, P)],
                                              src[:, g * GB + b:g * GB + b + 2, :].rearrange("p k f -> p (k f)"),
                                              ident[:, :])
                ins.then_inc(xt_ready, 1)
                pe.wait_ge(xt_copied, n + 1)
                for b in range(GB // 2):
                    ins = nc.tensor.matmul(banks[2 * (n % 2) + 1][:, bass.ts(b, 2 * width)],
                                           x_t[n % 2][:, bass.ts(b, P)], w[:, :, :].rearrange("p b f -> p (b f)"),
                                           start=True, stop=True)
                ins.then_inc(u_ready, 1)

            pe.wait_ge(const_loaded, 96)
            for layer, (w, width, pair, first_bank) in enumerate([(w2_s, 2 * F, pair2, 6), (w3_s, F, pair3, 4)]):
                base = layer * NG
                project(base, w, width)
                for g in range(NG):
                    if g + 1 < NG:
                        project(base + g + 1, w, width)
                    pe.wait_ge(u_read, base + g + 1)
                    for k in range(g * GB, g * GB + GB):
                        ins = aggregate(first_bank, pair, k)
                ins.then_inc(acc_ready, 1)


def kernel(x, adj, L0_gnn_theta, L0_gnn_W, L0_gnn_b, L1_gnn_t, L2_gnn_W, L2_gnn_b, L3_gnn_weight):
    import numpy as np
    import concourse.bacc as bacc
    from concourse.bass_utils import run_bass_kernel_spmd

    x, adj, w0, w2 = np.asarray(x), np.asarray(adj), np.asarray(L0_gnn_W), np.asarray(L2_gnn_W)
    n, f = x.shape
    arrays = {
        "xT": np.ascontiguousarray(x.T),
        "x": x,
        "adj": adj,
        "theta": np.asarray(L0_gnn_theta),
        "w0T": np.ascontiguousarray(w0.T),
        "b0": np.asarray(L0_gnn_b),
        "w2": np.ascontiguousarray(np.concatenate([w2[:f], w2[f:]], axis=1)),
        "b2": np.asarray(L2_gnn_b),
        "w3": np.asarray(L3_gnn_weight),
    }
    nc = bacc.Bacc("TRN2", target_bir_lowering=False, num_devices=1)
    args = [nc.dram_tensor(name, a.shape, mybir.dt.from_np(a.dtype), kind="ExternalInput").ap()
            for name, a in arrays.items()]
    xw = nc.dram_tensor("xw", (n, f), F32, kind="Internal").ap()
    out = nc.dram_tensor("out", (n, f), F32, kind="ExternalOutput").ap()
    graph_layers(nc, *args, xw, out)
    r = run_bass_kernel_spmd(nc, [arrays], core_ids=[0])
    return r.results[0]["out"]
```

```python
from contextlib import ExitStack

import concourse.bass as bass
from concourse import mybir


ALU = mybir.AluOpType
ACT = mybir.ActivationFunctionType
AX = mybir.AxisListType
F32 = mybir.dt.float32
F16 = mybir.dt.float16
U32 = mybir.dt.uint32

P = 128
A_SCALE = 2.0 ** 12
R_SCALE = 2.0 ** 14
V_SCALE = 2.0 ** 10
EPS = 1e-5
HI, LO = 0, 1


def wait_apart(eng, sem, value):
    if not isinstance(value, int):
        value = eng.to_reg(value)
        eng.wait_ge(sem, 1)
    eng.wait_ge(sem, value)


class Steps:

    def __init__(self, eng, sem):
        self.eng, self.sem, self.base, self.n = eng, sem, 0, 0

    def done(self, ins):
        ins.then_inc(self.sem, 1)
        self.n += 1

    def settle(self):
        self.eng.wait_ge(self.sem, self.base + self.n)

    def link(self, ins):
        self.done(ins)
        self.settle()

    def settle_apart(self):
        wait_apart(self.eng, self.sem, self.base + self.n)

    def link_apart(self, ins):
        self.done(ins)
        self.settle_apart()

    def enter(self, turn, per):
        self.start, self.per = self.base + self.n, per
        self.base, self.n = self.start + turn * per, 0

    def leave(self, turns):
        assert self.n == self.per, self.n
        self.base, self.n = self.start + turns * self.per, 0


def graph_layers(nc, xT, x, adj, adjT, tables, theta, w0T, b0, w2, b2, w3, xw_dram, r_dram, out):
    N, F = x.shape
    KB = N // P
    CW = 512
    CH = N // CW
    DIAG = CW // P
    TOP = 4
    UNIT = 4
    LISTED = UNIT * P
    LAG = 2
    GB = 4
    NG = KB // GB
    FAR = 4096.0

    with ExitStack() as ctx:
        def sb(name, shape, dt):
            return ctx.enter_context(nc.sbuf_tensor(name, shape, dt))

        def sem(name):
            return ctx.enter_context(nc.semaphore(name))

        at = sb("at", [P, 2, KB, N], F16)
        slots = sb("slots", [P, UNIT + 1, 2, N], F16)
        row = sb("row", [P, N], F32)
        g_bc = sb("g_bc", [P, N], F32)
        listed_f = sb("listed_f", [P, UNIT, P], F32)
        listed = sb("listed", [P, UNIT, 2, P], F16)
        xb = sb("xb", [P, KB, F], F32)
        x1 = sb("x1", [P, KB, F], F32)
        x1_pair = sb("x1_pair", [P, KB, 2, F], F16)
        node16 = sb("node16", [P, KB], F16)
        list_r = sb("list_r", [P, KB * KB], U32)
        list_at = sb("list_at", [P, KB * KB], U32)
        pick_r = sb("pick_r", [P, UNIT], U32)
        pick_at = sb("pick_at", [P, UNIT], U32)
        more_units = sb("more_units", [P, 1], U32)
        gathered = sb("gathered", [P, TOP, F], F32)
        y0 = sb("y0", [P, F], F32)
        ident = sb("ident", [P, P], F32)
        ident16 = sb("ident16", [P, P], F16)
        ones16 = sb("ones16", [P, P], F16)
        w2_s = sb("w2_s", [P, 2, 2 * F], F32)
        w3_s = sb("w3_s", [P, 2, F], F32)
        bias2 = sb("bias2", [P, F], F32)
        th = sb("th", [P, 2], F32)
        t01 = sb("t01", [P, 2], F32)
        t1_scaled = sb("t1_scaled", [P, 1], F32)
        t0_scaled = sb("t0_scaled", [P, 1], F32)
        d_scaled = sb("d_scaled", [P, KB], F32)
        c_row = sb("c_row", [P, KB], F32)
        dinv = sb("dinv", [P, KB], F32)
        droot = sb("droot", [P, KB], F32)
        vec = sb("vec", [P, KB], F32)
        vec16 = sb("vec16", [P, KB, 2], F16)
        mv_s = sb("mv_s", [P, KB, 2], F32)
        u_s = sb("u_s", [P, KB], F32)
        d2 = sb("d2", [P, KB], F32)
        dinv2 = sb("dinv2", [P, KB], F32)
        g_col = sb("g_col", [P, KB], F32)
        g_hi = sb("g_hi", [P, KB], F16)
        g_out = sb("g_out", [P, KB], F32)
        q_col = sb("q_col", [P, KB], F32)
        rdeg = sb("rdeg", [P, KB], F32)
        eps_s = sb("eps_s", [P, 1], F32)
        one_s = sb("one_s", [P, 1], F32)
        best = sb("best", [P, 8], F32)
        next_best = sb("next_best", [P, 8], F32)
        next_idx = sb("next_idx", [P, 8], U32)
        gather_idx = sb("gather_idx", [P, TOP], U32)
        stats = sb("stats", [P, GB, 6], F32)
        moments = sb("moments", [P, 2, GB, 2], F32)
        sd = sb("sd", [P, 2, GB], F32)
        rs = sb("rs", [P, 2, GB], F32)
        shift = sb("shift", [P, 2, GB], F32)
        red = sb("red", [P, GB], F32)

        banks = [ctx.enter_context(nc.psum_tensor(f"bank{i}", [P, 512], F32)) for i in range(8)]
        FLAGS, COUNTS, VEC, POS = banks[5], banks[4], banks[6], banks[7]
        LISTS = banks[5]
        XW = [banks[6], banks[7]]

        def flat(t):
            return t.rearrange("p u n -> p (u n)")

        rows = [flat(slots[:, u]).bitcast(F32) for u in range(2)]
        nat = [slots[:, 2 + u] for u in range(2)]
        r_out = [slots[:, UNIT], row[:, :].bitcast(F16).rearrange("p (u n) -> p u n", u=2)]
        xT_s = g_bc[0:F, :]
        t0_diag, own_t = listed_f[:, 2, :], listed_f[:, 3, :]
        tri, iota16 = listed[:, 0, HI, :], listed[:, 0, LO, :]
        w0_s = x1_pair[0:F, 0:2, :, :].rearrange("p a b f -> p (a b f)")[:, 0:2 * F].bitcast(F32)
        bias0 = gathered[:, 1, :]
        h0 = gathered[:, 0, :]
        xw_s = x1[:, :, :]
        g_diag = row[:, :].bitcast(F16).rearrange("p (q u k c) -> p q u k c", q=CH, u=2, c=P)
        HALF = KB // 2
        NT = P + P + KB * KB + KB
        tables_s = g_bc[:, 0:NT]
        tri_f, iota_f = tables_s[:, 0:P], tables_s[:, P:2 * P]
        base_f, node_f = tables_s[:, 2 * P:2 * P + KB * KB], tables_s[:, 2 * P + KB * KB:NT]
        lower_w, upper_w = 3 * HALF * P // 2, 3 * HALF * KB // 2
        lower = row[:, 0:lower_w].bitcast(F16).rearrange("p (h k c) -> p h k c", h=3, c=P)
        upper = row[:, lower_w:lower_w + upper_w].bitcast(F16).rearrange("p (h k c) -> p h k c", h=3, c=KB)
        at_tab = [NT]

        def tab(width):
            at_tab[0] += width
            return g_bc[:, at_tab[0] - width:at_tab[0]]

        flags16 = tab(KB * KB // 2).bitcast(F16)
        pos_f = tab(KB * KB)
        upper16 = tab(KB * KB // 2).bitcast(F16)
        lower16 = tab(KB * KB // 2).bitcast(F16)
        number_f = tab(KB * KB)
        assert at_tab[0] <= N
        place_f = listed_f[:, 0:2, :].rearrange("p b c -> p (b c)")

        end = slots[:, :, :, :].rearrange("p a b c -> p (a b c)").bitcast(F32)
        at_end = [0]

        def carve(width):
            at_end[0] += width
            return end[:, at_end[0] - width:at_end[0]]

        def carve_nodes():
            return carve(KB * F).rearrange("p (k f) -> p k f", f=F)

        x2, x3, x1_part = carve_nodes(), carve_nodes(), carve_nodes()
        u_top, u_bot, z_part = carve_nodes(), carve_nodes(), carve_nodes()
        pair2 = carve(KB * F).bitcast(F16).rearrange("p (k u f) -> p k u f", u=2, f=F)
        pair3 = carve(KB * F).bitcast(F16).rearrange("p (k u f) -> p k u f", u=2, f=F)
        ta = carve(GB * F).rearrange("p (k f) -> p k f", f=F)
        tb = carve(GB * F).rearrange("p (k f) -> p k f", f=F)
        x_t = [carve(GB * F) for _ in range(2)]
        x4 = carve_nodes()

        const_loaded = sem("const_loaded")
        xw_in_loaded = sem("xw_in_loaded")
        xb_loaded = sem("xb_loaded")
        rows_loaded = [sem("rows_loaded0"), sem("rows_loaded1")]
        tables_loaded = sem("tables_loaded")
        tables_ready = sem("tables_ready")
        w_zeroed = sem("w_zeroed")
        xw_ready = sem("xw_ready")
        xw_copied = sem("xw_copied")
        xw_stored = sem("xw_stored")
        pool_step = sem("pool_step")
        ident_ready = sem("ident_ready")
        exp_done = sem("exp_done")
        t_ready = sem("t_ready")
        hi_ready = sem("hi_ready")
        lo_ready = sem("lo_ready")
        c_ready = sem("c_ready")
        rhi_ready = sem("rhi_ready")
        r_ready = sem("r_ready")
        r_stored = [sem("r_stored0"), sem("r_stored1")]
        tp_ready = [sem(f"tp_ready{t}") for t in range(4)]
        tp_evac = [sem(f"tp_evac{t}") for t in range(4)]
        flags_ready = sem("flags_ready")
        pos_ready = sem("pos_ready")
        tables_copied = sem("tables_copied")
        places_ready = sem("places_ready")
        onehot_dve = sem("onehot_dve")
        onehot_act = sem("onehot_act")
        act_step = sem("act_step")
        onehot_used = sem("onehot_used")
        units_ready = sem("units_ready")
        lists_ready = sem("lists_ready")
        r_loaded = [sem(f"r_loaded{b}") for b in range(UNIT)]
        listed_loaded = [sem(f"listed_loaded{b}") for b in range(UNIT)]
        listed_hi = sem("listed_hi")
        listed_ready = sem("listed_ready")
        slot_used = [sem(f"slot_used{b}") for b in range(UNIT - 1)]
        own_loaded = sem("own_loaded")
        own_used = sem("own_used")
        tile_ready = sem("tile_ready")
        tile_evac = sem("tile_evac")
        row_used = sem("row_used")
        moments_ready = sem("moments_ready")
        sd_ready = sem("sd_ready")
        root_in = sem("root_in")
        root_out = sem("root_out")
        vec_ready = sem("vec_ready")
        mv_ready = sem("mv_ready")
        gdiag_ready = sem("gdiag_ready")
        gbank_ready = sem("gbank_ready")
        g_ready = sem("g_ready")
        idx_ready = sem("idx_ready")
        rows_gathered = sem("rows_gathered")
        x1_ready = sem("x1_ready")
        acc_ready = sem("acc_ready")
        x_ready = sem("x_ready")
        xt_ready = sem("xt_ready")
        xt_copied = sem("xt_copied")
        u_ready = sem("u_ready")
        u_evac = sem("u_evac")
        pair_ready = sem("pair_ready")
        shift_ready = sem("shift_ready")
        out_dve = sem("out_dve")
        out_act = sem("out_act")
        out_stored = sem("out_stored")
        dve_step = sem("dve_step")
        late_step = sem("late_step")

        def a_block(part, k, i):
            return at[:, part, k, bass.ts(i, P)]

        def row_block_of(v, units):
            i = v // units
            return i if isinstance(i, int) else i.with_bounds(min_val=0, max_val=KB - 1)

        def by_act(n):
            return n % 3 == 2

        def unit_count(eng):
            eng.wait_ge(units_ready, 1)
            return eng.value_load(more_units[0:1, 0:1], min_val=0, max_val=(KB - 1 + UNIT - 1) // UNIT - 1)

        block = ctx.enter_context(nc.Block())

        @block.sync
        def _(sp):
            sp.dma_start(rows[0], adj[0:P, :]).then_inc(rows_loaded[0], 16)
            sp.dma_start(th[:, :], theta.partition_broadcast(P)).then_inc(const_loaded, 16)
            sp.dma_start(rows[1], adj[P:2 * P, :]).then_inc(rows_loaded[1], 16)
            sp.dma_start(xT_s, xT).then_inc(xw_in_loaded, 16)
            sp.dma_start(w0_s, w0T).then_inc(xw_in_loaded, 16)
            sp.dma_start(xb[:, :, :], x.rearrange("(k p) f -> p k f", p=P)).then_inc(xb_loaded, 16)
            sp.dma_start(bias0, b0.partition_broadcast(P)).then_inc(xb_loaded, 16)

            def row_block(r, u, following=True):
                sp.wait_ge(r_ready, r + 1)
                if following:
                    sp.dma_start(rows[u], adj[bass.ds((r + 2) * P, P), :]).then_inc(rows_loaded[u], 16)
                sp.dma_start(r_dram[bass.ds(r * P, P), :], r_out[u].rearrange("p u n -> p (u n)")) \
                    .then_inc(r_stored[u], 16)

            row_block(0, 0)
            row_block(1, 1)
            sp.wait_ge(xw_copied, 2)
            sp.dma_start(xw_dram.rearrange("(k p) f -> p k f", p=P), xw_s).then_inc(xw_stored, 16)
            sp.dma_start(tables_s, tables).then_inc(tables_loaded, 16)
            sp.dma_start(bias2[:, :], b2.partition_broadcast(P)).then_inc(const_loaded, 16)
            sp.wait_ge(w_zeroed, 2)
            for half in range(2):
                sp.dma_start(w2_s[half * F:half * F + F, half, :], w2).then_inc(const_loaded, 16)
                sp.dma_start(w3_s[half * F:half * F + F, half, :], w3).then_inc(const_loaded, 16)
            with sp.Fori(1, KB // 2 - 1) as pair:
                row_block(pair * 2, 0)
                row_block(pair * 2 + 1, 1)
            row_block(KB - 2, 0, following=False)
            row_block(KB - 1, 1, following=False)
            sp.wait_ge(r_stored[0], 16 * KB // 2)
            sp.wait_ge(r_stored[1], 16 * KB // 2)
            own = slots[:, UNIT].rearrange("p u n -> p (u n)")
            sp.dma_start(own, r_dram[0:P, :]).then_inc(own_loaded, 16)
            with sp.Fori(1, KB) as i:
                sp.wait_ge(own_used, i)
                sp.dma_start(own, r_dram[bass.ds(i * P, P), :]).then_inc(own_loaded, 16)
            out_v = out.rearrange("(k p) f -> p k f", p=P)
            for g in range(NG):
                sp.wait_ge(out_dve, g + 1)
                sp.wait_ge(out_act, g + 1)
                sp.dma_start(out_v[:, g * GB:g * GB + GB, :], x4[:, g * GB:g * GB + GB, :]).then_inc(out_stored, 16)
            sp.wait_ge(out_stored, 16 * NG)

        @block.gpsimd
        def _(pool):
            nc.gpsimd.memset(ones16[:, :], 1.0).then_inc(pool_step, 1)
            pool.wait_ge(pool_step, 1)
            nc.gpsimd.affine_select(out=ident[:, :], in_=ones16[:, :], compare_op=ALU.is_equal, fill=0.0, base=0,
                                    pattern=[[-1, P]], channel_multiplier=1).then_inc(pool_step, 1)
            pool.wait_ge(pool_step, 2)
            nc.gpsimd.tensor_copy(ident16[:, :], ident[:, :]).then_inc(ident_ready, 1)
            nc.gpsimd.memset(w2_s[:, :, :], 0.0).then_inc(w_zeroed, 1)
            nc.gpsimd.memset(w3_s[:, :, :], 0.0).then_inc(w_zeroed, 1)

            pool.wait_ge(tables_loaded, 16)
            nc.gpsimd.tensor_copy(tri, tri_f).then_inc(tables_copied, 1)
            nc.gpsimd.tensor_copy(iota16, iota_f).then_inc(tables_copied, 1)
            nc.gpsimd.tensor_copy(node16[:, :], node_f).then_inc(tables_copied, 1)

            more = unit_count(pool)
            units, total = more + 1, more * KB + KB

            def gather_unit(v):
                first = isinstance(v, int) and v == 0
                slot0 = row_block_of(v, units) * KB + (v % units) * UNIT
                for b in range(UNIT):
                    if not first:
                        pool.wait_ge(listed_ready, v * UNIT + (b + 1 - UNIT))
                    nc.gpsimd.tensor_copy(pick_at[:, b:b + 1], list_at[:, bass.ds(slot0 + b, 1)]) \
                        .then_inc(pool_step, 1)
                    wait_apart(pool, pool_step, v * (2 * UNIT) + (2 * b + 3))
                    pool.indirect_dma_start(
                        out=listed_f[:, b, :], out_offset=None, in_=adjT,
                        in_offset=bass.IndirectOffsetOnAxis(ap=pick_at[:, b:b + 1], axis=0),
                    ).then_inc(listed_loaded[b], 16)
                    if not first:
                        if b < UNIT - 1:
                            pool.wait_ge(slot_used[b], v)
                        else:
                            pool.wait_ge(tile_ready, v * CH)
                    nc.gpsimd.tensor_copy(pick_r[:, b:b + 1], list_r[:, bass.ds(slot0 + b, 1)]) \
                        .then_inc(pool_step, 1)
                    wait_apart(pool, pool_step, v * (2 * UNIT) + (2 * b + 4))
                    pool.indirect_dma_start(
                        out=slots[:, b].rearrange("p u n -> p (u n)"), out_offset=None, in_=r_dram,
                        in_offset=bass.IndirectOffsetOnAxis(ap=pick_r[:, b:b + 1], axis=0),
                    ).then_inc(r_loaded[b], 16)

            def gather_best(v):
                wait_apart(pool, idx_ready, v + 1)
                for s in range(TOP):
                    pool.indirect_dma_start(
                        out=gathered[:, s, :], out_offset=None, in_=xw_dram,
                        in_offset=bass.IndirectOffsetOnAxis(ap=gather_idx[:, s:s + 1], axis=0),
                    ).then_inc(rows_gathered, 16)

            pool.wait_ge(lists_ready, 1)
            pool.wait_ge(xw_stored, 16)
            for u in range(2):
                pool.wait_ge(r_stored[u], 16 * KB // 2)
            pool.wait_ge(tp_ready[3], KB)
            gather_unit(0)
            pool.wait_ge(lists_ready, 2)
            gather_unit(1)
            with pool.Fori(2, total) as v:
                gather_unit(v)
                gather_best(v - 2)
            gather_best(more * KB + (KB - 2))
            gather_best(more * KB + (KB - 1))

        @block.scalar
        def _(act):
            act.wait_ge(const_loaded, 16)
            nc.scalar.activation(t01[:, :], th[:, :], ACT.Exp, scale=-1.0).then_inc(exp_done, 1)

            def row_block(r, u, turn):
                late = not (isinstance(r, int) and r < 2)
                act.wait_ge(rows_loaded[u], 16 * turn + 16)
                if late:
                    act.wait_ge(tp_ready[3], r - 1)
                nc.scalar.activation(nat[u][:, HI, :], rows[u], ACT.Copy, scale=A_SCALE,
                                     accum_out=d_scaled[:, bass.ds(r, 1)]).then_inc(hi_ready, 1)
                evacuate(r, 0)
                act.wait_ge(c_ready, r + 1)
                if late:
                    act.wait_ge(r_stored[u], 16 * turn)
                nc.scalar.activation(r_out[u][:, HI, :], rows[u], ACT.Copy, scale=c_row[:, bass.ds(r, 1)]) \
                    .then_inc(rhi_ready, 1)
                evacuate(r, 2)
                evacuate(r, 3)

            def evacuate(r, t):
                act.wait_ge(tp_ready[t], r + 1)
                half = t % 2 * KB // 2
                nc.scalar.copy(at[:, t // 2, half:half + KB // 2, bass.ds(r * P, P)],
                               banks[t][:, :].bitcast(F16).rearrange("p (k c) -> p k c", c=P)).then_inc(tp_evac[t], 1)

            row_block(0, 0, 0)
            row_block(1, 1, 0)
            for h in range(2):
                act.wait_ge(xw_ready, h + 1)
                nc.scalar.copy(xw_s[:, h * KB // 2:(h + 1) * KB // 2, :],
                               XW[h][:, :].rearrange("p (k f) -> p k f", f=F)).then_inc(xw_copied, 1)
            with act.Fori(1, KB // 2) as pair:
                row_block(pair * 2, 0, pair)
                row_block(pair * 2 + 1, 1, pair)

            act.wait_ge(root_in, 1)
            nc.scalar.activation(droot[:, :], u_s[:, :], ACT.Sqrt).then_inc(root_out, 1)
            more = unit_count(act)
            units, total = more + 1, more * KB + KB
            nc.scalar.copy(sd[:, 1, 0:1], eps_s[:, 0:1]).then_inc(tile_evac, CH)

            act.wait_ge(places_ready, 1)
            act_steps = 0
            for n in range(2 * KB):
                if by_act(n):
                    if n >= 3:
                        act.wait_ge(onehot_used, n - 2)
                    for k in range(HALF):
                        nc.scalar.activation(lower[:, n % 3, k, :], iota16, ACT.Square,
                                             bias=pos_f[:, n * HALF + k:n * HALF + k + 1]).then_inc(act_step, 1)
                    act_steps += HALF
                    act.wait_ge(act_step, act_steps)
                    nc.scalar.activation(lower[:, n % 3], lower[:, n % 3], ACT.Relu, bias=one_s[:, 0:1], scale=-1.0) \
                        .then_inc(onehot_act, 1)

            act.wait_ge(root_in, 2)
            nc.scalar.activation(dinv2[:, :], d2[:, :], ACT.Sqrt).then_inc(root_out, 1)
            act.wait_ge(lists_ready, 2)
            for q in range(CH):
                act.wait_ge(gbank_ready, q + 1)
                nc.scalar.mul(g_bc[:, bass.ts(q, CW)], VEC[:, :], 1.0 / V_SCALE).then_inc(g_ready, 1)

            def split_listed(v, b):
                if not (isinstance(v, int) and v == 0):
                    if b < UNIT - 1:
                        act.wait_ge(slot_used[b], v)
                    else:
                        act.wait_ge(tile_ready, v * CH)
                act.wait_ge(listed_loaded[b], v * 16 + 16)
                nc.scalar.activation(listed[:, b, HI, :], listed_f[:, b, :], ACT.Copy, scale=A_SCALE) \
                    .then_inc(listed_hi, 1)

            def evacuate_row(v):
                if not (isinstance(v, int) and v == 0):
                    act.wait_ge(row_used, v)
                for c in range(CH):
                    act.wait_ge(tile_ready, v * CH + (c + 1))
                    nc.scalar.copy(row[:, bass.ts(c, CW)], banks[c][:, :]).then_inc(tile_evac, 1)

            def unit(v, after_first=True):
                for b in range(UNIT - 1):
                    split_listed(v + 1, b)
                evacuate_row(v)
                split_listed(v + 1, UNIT - 1)
                if after_first:
                    deviation0(v - 1)

            def deviation0(v):
                act.wait_ge(moments_ready, v + 1)
                nc.scalar.activation(sd[:, 0, 0:1], moments[:, 0, 0, 1:2], ACT.Sqrt, bias=eps_s[:, 0:1]) \
                    .then_inc(sd_ready, 1)

            for b in range(UNIT):
                split_listed(0, b)
            unit(0, after_first=False)
            with act.Fori(1, more * KB + (KB - 1)) as v:
                unit(v)
            deviation0(more * KB + (KB - 2))
            deviation0(more * KB + (KB - 1))

            roots = [2]

            def root(out_ap, in_ap, bias_ap=0.0):
                roots[0] += 1
                act.wait_ge(root_in, roots[0])
                nc.scalar.activation(out_ap, in_ap, ACT.Sqrt, bias=bias_ap).then_inc(root_out, 1)

            def deviation(n):
                root(sd[:, n % 2, :], moments[:, n % 2, :, 1], eps_s[:, 0:1])

            def turn_features(n):
                act.wait_ge(xt_ready, n + 1)
                nc.scalar.copy(x_t[n % 2], banks[2 * (n % 2)][:, 0:GB * F]).then_inc(xt_copied, 1)

            def evacuate_features(n, parts):
                act.wait_ge(u_ready, n + 1)
                g, width = n % NG, F * len(parts)
                u = banks[2 * (n % 2) + 1][:, 0:GB * width].rearrange("p (k f) -> p k f", f=width)
                for at_f, dst in parts:
                    nc.scalar.copy(dst[:, g * GB:g * GB + GB, :], u[:, :, at_f:at_f + F]).then_inc(u_evac, 1)

            deviation(0)
            for g in range(NG):
                turn_features(g)
                if g + 1 < NG:
                    deviation(g + 1)
                evacuate_features(g, [(F, u_bot), (0, u_top)])
            for g in range(NG):
                root(red[:, :], red[:, :])
                deviation(NG + g)
                if g:
                    evacuate_features(NG + g - 1, [(0, u_bot)])
                turn_features(NG + g)
            evacuate_features(2 * NG - 1, [(0, u_bot)])

            def last_norm(g):
                act.wait_ge(shift_ready, g + 1)
                n = (2 * NG + g) % 2
                for b in range(GB // 2, GB):
                    ins = nc.scalar.activation(x4[:, g * GB + b, :], [ta, tb][n][:, b, :], ACT.Identity,
                                               bias=shift[:, n, b:b + 1], scale=rs[:, n, b:b + 1])
                ins.then_inc(out_act, 1)

            deviation(2 * NG)
            for g in range(NG):
                if g + 1 < NG:
                    deviation(2 * NG + g + 1)
                last_norm(g)

        @block.vector
        def _(dve):
            step = Steps(dve, dve_step)
            link = step.link
            roots = [0]

            def row_block(r, u, turn):
                late = not (isinstance(r, int) and r < 2)
                dve.wait_ge(hi_ready, r + 1)
                scale = c_row[:, bass.ds(r, 1)]
                link(nc.vector.reciprocal(scale, d_scaled[:, bass.ds(r, 1)]))
                nc.vector.tensor_scalar(scale, scale, t1_scaled[:, 0:1], None, ALU.mult).then_inc(c_ready, 1)
                nc.vector.scalar_tensor_tensor(nat[u][:, LO, :], rows[u], A_SCALE, nat[u][:, HI, :],
                                               ALU.mult, ALU.subtract).then_inc(lo_ready, 1)
                evacuate(r, 1)
                dve.wait_ge(rhi_ready, r + 1)
                dve.wait_ge(c_ready, r + 1)
                step.done(nc.vector.scalar_tensor_tensor(r_out[u][:, LO, :], rows[u], scale, r_out[u][:, HI, :],
                                                         ALU.mult, ALU.subtract))
                own = bass.ds(r * P, P)
                step.link(nc.vector.scalar_tensor_tensor(own_t, rows[u][:, own], scale, t0_diag,
                                                         ALU.mult, ALU.add))
                link(nc.vector.tensor_copy(r_out[u][:, HI, own], own_t))
                nc.vector.tensor_tensor(r_out[u][:, LO, own], own_t, r_out[u][:, HI, own],
                                        ALU.subtract).then_inc(r_ready, 1)
                dve.wait_ge(r_ready, r + 1)

            def evacuate(r, t):
                dve.wait_ge(tp_ready[t], r + 1)
                nc.vector.tensor_copy(at[:, t // 2, KB // 2:KB, bass.ds(r * P, P)],
                                      banks[t][:, :].bitcast(F16).rearrange("p (k c) -> p k c", c=P)) \
                    .then_inc(tp_evac[t], 1)

            nc.vector.memset(eps_s[:, :], EPS)
            nc.vector.memset(one_s[:, :], 1.0)
            dve.wait_ge(exp_done, 1)
            link(nc.vector.tensor_scalar(t01[:, :], t01[:, :], 1.0, None, ALU.add))
            link(nc.vector.reciprocal(t01[:, :], t01[:, :]))
            link(nc.vector.tensor_scalar(t1_scaled[:, :], t01[:, 1:2], A_SCALE * R_SCALE, None, ALU.mult))
            link(nc.vector.tensor_scalar(t0_scaled[:, :], t01[:, 0:1], R_SCALE, None, ALU.mult))
            dve.wait_ge(ident_ready, 1)
            link(nc.vector.tensor_scalar(t0_diag, ident[:, :], t0_scaled[:, 0:1], None, ALU.mult))

            row_block(0, 0, 0)
            row_block(1, 1, 0)
            with dve.Fori(1, KB // 2) as pair:
                step.enter(pair - 1, 8)
                row_block(pair * 2, 0, pair)
                row_block(pair * 2 + 1, 1, pair)
                step.leave(KB // 2 - 1)

            def root(value):
                value.then_inc(root_in, 1)
                roots[0] += 1

            def wait_root():
                dve.wait_ge(root_out, roots[0])

            def split_vec():
                link(nc.vector.tensor_scalar(vec[:, :], vec[:, :], V_SCALE, None, ALU.mult))
                link(nc.vector.tensor_copy(vec16[:, :, HI], vec[:, :]))
                nc.vector.tensor_tensor(vec16[:, :, LO], vec[:, :], vec16[:, :, HI], ALU.subtract) \
                    .then_inc(vec_ready, 1)

            def matvec_out(n):
                dve.wait_ge(mv_ready, n + 1)
                link(nc.vector.tensor_copy(mv_s[:, :, :], VEC[:, 0:2 * KB].rearrange("p (k t) -> p k t", t=2)))
                link(nc.vector.tensor_tensor(vec[:, :], mv_s[:, :, 0], mv_s[:, :, 1], ALU.add))
                link(nc.vector.tensor_scalar(vec[:, :], vec[:, :], 1.0 / (A_SCALE * V_SCALE), None, ALU.mult))

            root(nc.vector.tensor_scalar(u_s[:, :], d_scaled[:, :], 1.0 / A_SCALE, None, ALU.mult))
            dve.wait_ge(root_in, 1)
            link(nc.vector.tensor_scalar(rdeg[:, :], u_s[:, :], 1.0, 1.0, ALU.add, ALU.max))
            link(nc.vector.reciprocal(rdeg[:, :], rdeg[:, :]))
            wait_root()
            link(nc.vector.reciprocal(dinv[:, :], droot[:, :]))
            link(nc.vector.tensor_copy(vec[:, :], dinv[:, :]))
            split_vec()

            dve.wait_ge(tables_copied, 3)
            dve.wait_ge(flags_ready, 1)
            link(nc.vector.tensor_scalar(flags16, FLAGS[:, 0:KB * KB], 0.0, None, ALU.is_gt))
            step.done(nc.vector.memset(flags16[:, 0:KB * KB:KB + 1], 0.0))
            step.settle()
            nc.vector.tensor_scalar(pos_f, flags16, -FAR, FAR, ALU.mult, ALU.add).then_inc(tables_ready, 1)
            dve.wait_ge(tables_ready, 1)
            dve.wait_ge(pos_ready, 1)
            link(nc.vector.tensor_tensor(pos_f, pos_f, POS[:, 0:KB * KB], ALU.add))
            link(nc.vector.tensor_reduce(u_s[:, :], COUNTS[:, 0:KB * KB].rearrange("p (r k) -> p r k", k=KB),
                                         AX.X, ALU.add))
            link(nc.vector.tensor_reduce(red[:, 0:1], u_s[:, :], AX.X, ALU.max))
            link(nc.vector.tensor_scalar(red[:, 1:2], red[:, 0:1], float(LISTED), None, ALU.is_gt))
            for n in range(2, (KB - 1 + UNIT - 1) // UNIT):
                link(nc.vector.tensor_scalar(red[:, 2:3], red[:, 0:1], float(LISTED * n), None, ALU.is_gt))
                link(nc.vector.tensor_tensor(red[:, 1:2], red[:, 1:2], red[:, 2:3], ALU.add))
            nc.vector.tensor_copy(more_units[:, :], red[:, 1:2]).then_inc(units_ready, 1)
            link(nc.vector.tensor_scalar(place_f, pos_f, 1.0 / P, -0.498, ALU.mult, ALU.add))
            link(nc.vector.tensor_scalar(place_f, place_f, 1.5 * 2.0 ** 23, None, ALU.add))
            link(nc.vector.tensor_scalar(place_f, place_f, -1.5 * 2.0 ** 23, None, ALU.add))
            link(nc.vector.scalar_tensor_tensor(lower16, place_f, -float(P), pos_f, ALU.mult, ALU.add))

            def evacuate_lists(half):
                dve.wait_ge(onehot_used, KB * (half + 1))
                cols = slice(half * KB * HALF, (half + 1) * KB * HALF)
                link(nc.vector.tensor_scalar(number_f[:, cols], LISTS[:, cols], 0.0, node_f[:, 0:1],
                                             ALU.is_equal, ALU.mult))
                link(nc.vector.tensor_tensor(number_f[:, cols], number_f[:, cols], LISTS[:, cols], ALU.add))
                link(nc.vector.tensor_scalar(list_r[:, cols], number_f[:, cols], -1.0, None, ALU.add))
                nc.vector.tensor_tensor(list_at[:, cols], LISTS[:, cols], base_f[:, cols], ALU.add) \
                    .then_inc(lists_ready, 1)

            def onehots(n):
                h, buf, cols = n % 2, n % 3, slice(n * HALF, n * HALF + HALF)
                if n >= 3:
                    dve.wait_ge(onehot_used, n - 2)
                link(nc.vector.tensor_tensor(upper[:, buf], iota16[:, 0:KB].unsqueeze(1).to_broadcast([P, HALF, KB]),
                                             upper16[:, cols].unsqueeze(2).to_broadcast([P, HALF, KB]),
                                             ALU.is_equal))
                ins = nc.vector.tensor_tensor(upper[:, buf], upper[:, buf],
                                              node16[:, h * HALF:h * HALF + HALF].unsqueeze(2)
                                              .to_broadcast([P, HALF, KB]), ALU.mult)
                if not by_act(n):
                    step.done(ins)
                    ins = nc.vector.tensor_tensor(lower[:, buf], iota16.unsqueeze(1).to_broadcast([P, HALF, P]),
                                                  lower16[:, cols].unsqueeze(2).to_broadcast([P, HALF, P]),
                                                  ALU.is_equal)
                ins.then_inc(onehot_dve, 1)

            dve.wait_ge(r_stored[1], 16 * KB // 2)
            link(nc.vector.tensor_copy(upper16, place_f))
            nc.vector.tensor_scalar(pos_f, lower16, -1.0, None, ALU.mult).then_inc(places_ready, 1)
            for n in range(KB):
                onehots(n)
            evacuate_lists(0)
            matvec_out(0)
            link(nc.vector.tensor_tensor(u_s[:, :], vec[:, :], dinv[:, :], ALU.mult))
            link(nc.vector.tensor_tensor(vec[:, :], u_s[:, :], dinv[:, :], ALU.mult))
            split_vec()
            for n in range(KB, 2 * KB):
                onehots(n)
            evacuate_lists(1)
            matvec_out(1)
            link(nc.vector.tensor_tensor(vec[:, :], vec[:, :], dinv[:, :], ALU.mult))
            link(nc.vector.tensor_scalar(d2[:, :], u_s[:, :], t01[:, 0:1], 1.0, ALU.mult, ALU.add))
            root(nc.vector.scalar_tensor_tensor(d2[:, :], vec[:, :], t01[:, 1:2], d2[:, :], ALU.mult, ALU.add))
            wait_root()
            link(nc.vector.reciprocal(dinv2[:, :], dinv2[:, :]))
            link(nc.vector.tensor_tensor(g_col[:, :], dinv[:, :], dinv2[:, :], ALU.mult))
            step.done(nc.vector.tensor_scalar(g_out[:, :], g_col[:, :], 1.0 / (A_SCALE * R_SCALE), None, ALU.mult))
            link(nc.vector.scalar_tensor_tensor(q_col[:, :], dinv2[:, :], A_SCALE * R_SCALE, droot[:, :],
                                                ALU.mult, ALU.mult))
            link(nc.vector.tensor_scalar(vec[:, :], g_col[:, :], V_SCALE, None, ALU.mult))
            link(nc.vector.tensor_copy(g_hi[:, :], vec[:, :]))
            link(nc.vector.tensor_tensor(u_s[:, :], vec[:, :], g_hi[:, :], ALU.subtract))

            def spread_g(q):
                blocks = slice(q * DIAG, q * DIAG + DIAG)
                for part, g in ((HI, vec), (LO, u_s)):
                    ins = nc.vector.tensor_tensor(g_diag[:, q, part],
                                                  ident[:, :].unsqueeze(1).to_broadcast([P, DIAG, P]),
                                                  g[:, blocks].unsqueeze(2).to_broadcast([P, DIAG, P]), ALU.mult)
                    ins.then_inc(gdiag_ready, 1)

            spread_g(0)
            dve.wait_ge(xb_loaded, 32)
            link(nc.vector.tensor_tensor(xb[:, :, :], xb[:, :, :],
                                         bias0.unsqueeze(1).to_broadcast([P, KB, F]), ALU.add))
            for q in range(1, CH):
                spread_g(q)

            def measure(n, h):
                for b in range(len(h)):
                    step.done(nc.vector.bn_stats(stats[:, b, :], h[b]))
                step.settle_apart()
                for b in range(len(h)):
                    ins = nc.vector.bn_aggr(moments[:, n, b, :], stats[:, b, :])
                    if b < len(h) - 1:
                        step.done(ins)
                return ins

            more = unit_count(dve)
            units, total = more + 1, more * KB + KB

            def split_listed(v, b):
                dve.wait_ge(listed_hi, v * UNIT + (b + 1))
                nc.vector.scalar_tensor_tensor(listed[:, b, LO, :], listed_f[:, b, :], A_SCALE, listed[:, b, HI, :],
                                               ALU.mult, ALU.subtract).then_inc(listed_ready, 1)

            def scale_row(v):
                i = row_block_of(v, units)
                dve.wait_ge(tile_evac, v * CH + 2 * CH)
                link(nc.vector.tensor_tensor(row[:, :], row[:, :], g_bc[:, :], ALU.mult))
                own = bass.ds(i * P, P)
                step.done(nc.vector.scalar_tensor_tensor(row[:, own], ident[:, :], q_col[:, bass.ds(i, 1)], row[:, own],
                                                    ALU.mult, ALU.add))

            def select(v):
                step.link_apart(nc.vector.max(next_best[:, :], row[:, :]))
                nc.vector.max_index(next_idx[:, :], next_best[:, :], row[:, :]).then_inc(row_used, 1)

            def hand_over(v):
                dve.wait_ge(row_used, v + 1)
                step.done(nc.vector.tensor_copy(best[:, :], next_best[:, :]))
                nc.vector.tensor_copy(gather_idx[:, :], next_idx[:, 0:TOP]).then_inc(idx_ready, 1)

            def finish(v):
                i = row_block_of(v, units)
                dve.wait_ge(rows_gathered, v * 64 + 64)
                step.settle()
                link(nc.vector.tensor_tensor(gathered[:, :, :], gathered[:, :, :],
                                             best[:, 0:TOP].unsqueeze(2).to_broadcast([P, TOP, F]), ALU.mult))
                link(nc.vector.tensor_reduce(y0[:, :], gathered[:, :, :].rearrange("p s f -> p f s"), AX.X, ALU.add))
                link(nc.vector.scalar_tensor_tensor(h0, y0[:, :], g_out[:, bass.ds(i, 1)],
                                                    xb[:, bass.ds(i, 1), :].squeeze(1), ALU.mult, ALU.add))
                measure(0, [h0]).then_inc(moments_ready, 1)
                dve.wait_ge(sd_ready, v + 1)
                link(nc.vector.reciprocal(rs[:, 0, 0:1], sd[:, 0, 0:1]))
                link(nc.vector.tensor_scalar(x1[:, bass.ds(i, 1), :].squeeze(1), h0, moments[:, 0, 0, 0:1],
                                             rs[:, 0, 0:1], ALU.subtract, ALU.mult))
                link(nc.vector.tensor_scalar(x1_pair[:, bass.ds(i, 1), HI, :].squeeze(1),
                                             x1[:, bass.ds(i, 1), :].squeeze(1), V_SCALE, None, ALU.mult))
                nc.vector.scalar_tensor_tensor(x1_pair[:, bass.ds(i, 1), LO, :].squeeze(1),
                                               x1[:, bass.ds(i, 1), :].squeeze(1), V_SCALE,
                                               x1_pair[:, bass.ds(i, 1), HI, :].squeeze(1),
                                               ALU.mult, ALU.subtract).then_inc(x1_ready, 1)

            def unit(v, after_first=True):
                for b in range(UNIT - 1):
                    split_listed(v + 1, b)
                scale_row(v)
                split_listed(v + 1, UNIT - 1)
                step.settle_apart()
                select(v)
                if after_first:
                    finish(v - 1)
                hand_over(v)

            for b in range(UNIT):
                split_listed(0, b)
            dve.wait_ge(g_ready, CH)
            unit(0, after_first=False)
            with dve.Fori(1, more * KB + (KB - 1)) as v:
                step.enter(v - 1, 11)
                unit(v)
                step.leave(more * KB + (KB - 2))
            finish(more * KB + (KB - 2))
            for c in range(CH):
                dve.wait_ge(tile_ready, total * CH - (CH - 1 - c))
                step.done(nc.vector.tensor_tensor(row[:, bass.ts(c, CW)], banks[c][:, :], g_bc[:, bass.ts(c, CW)],
                                                  ALU.mult))
            step.settle()
            own = bass.ts(KB - 1, P)
            step.done(nc.vector.scalar_tensor_tensor(row[:, own], ident[:, :], q_col[:, KB - 1:KB], row[:, own],
                                                     ALU.mult, ALU.add))
            step.settle_apart()
            select(total - 1)
            hand_over(total - 1)
            finish(more * KB + (KB - 1))
            step = Steps(dve, late_step)
            link = step.link
            dve.wait_ge(x1_ready, total)
            link(nc.vector.tensor_scalar(x1_part, x1[:, :, :], 0.9, 1.0, ALU.mult, ALU.add))

            def group(t, g):
                return t[:, g * GB:g * GB + GB, :]

            def spread(col):
                return col.unsqueeze(2).to_broadcast([P, GB, F])

            asked = [0]

            def ask_deviation(h):
                root(measure(asked[0] % 2, [h[:, b, :] for b in range(GB)]))
                asked[0] += 1

            def norm_group(dst, h, signal, count):
                n = (asked[0] - 1) % 2
                wait_root()
                link(nc.vector.reciprocal(rs[:, n, :], sd[:, n, :]))
                for b in range(GB):
                    ins = nc.vector.tensor_scalar(dst[:, b, :], h[:, b, :], moments[:, n, b, 0:1], rs[:, n, b:b + 1],
                                                  ALU.subtract, ALU.mult)
                    if b < GB - 1:
                        step.done(ins)
                ins.then_inc(signal, 1)
                dve.wait_ge(signal, count)

            unscale = 1.0 / (A_SCALE * V_SCALE)

            def acc(layer, g):
                dve.wait_ge(acc_ready, 2 * layer + g // (NG // 2) + 1)
                return banks[[4, 6, 4][layer] + g * GB * F // 512][:, (g * GB * F) % 512:(g * GB * F) % 512 + GB * F] \
                    .rearrange("p (k f) -> p k f", f=F)

            def feature_pair(n, pair, evacuations):
                g = n % NG
                dve.wait_ge(u_evac, evacuations)
                link(nc.vector.tensor_scalar(group(pair[:, :, HI, :], g), group(u_bot, g), V_SCALE, None, ALU.mult))
                nc.vector.scalar_tensor_tensor(group(pair[:, :, LO, :], g), group(u_bot, g), V_SCALE,
                                               group(pair[:, :, HI, :], g), ALU.mult, ALU.subtract) \
                    .then_inc(pair_ready, 1)

            for g in range(NG):
                link(nc.vector.scalar_tensor_tensor(ta, acc(0, g), unscale, group(x1, g), ALU.mult, ALU.mult))
                link(nc.vector.tensor_reduce(red[:, :], ta, AX.X, ALU.add))
                link(nc.vector.scalar_tensor_tensor(ta, spread(red[:, :]), -0.01, group(x1_part, g),
                                                    ALU.mult, ALU.add))
                ask_deviation(ta)
                if g:
                    feature_pair(g - 1, pair2, 2 * g - 1)
                norm_group(group(x2, g), ta, x_ready, g + 1)
            feature_pair(NG - 1, pair2, 2 * NG - 1)

            dve.wait_ge(const_loaded, 96)
            dve.wait_ge(u_evac, 2 * NG)
            for g in range(NG):
                step.done(nc.vector.tensor_tensor(group(z_part, g), group(u_bot, g),
                                                  spread(rdeg[:, g * GB:g * GB + GB]), ALU.mult))
                link(nc.vector.tensor_tensor(group(u_top, g), group(u_top, g),
                                             bias2[:, :].unsqueeze(1).to_broadcast([P, GB, F]), ALU.add))
                link(nc.vector.tensor_tensor(group(z_part, g), group(z_part, g), group(u_top, g), ALU.add))
            dve.wait_ge(pair_ready, NG)
            link(nc.vector.tensor_scalar(rdeg[:, :], rdeg[:, :], unscale, None, ALU.mult))
            for g in range(NG):
                link(nc.vector.tensor_tensor(ta, acc(1, g), spread(rdeg[:, g * GB:g * GB + GB]), ALU.mult))
                link(nc.vector.tensor_tensor(ta, ta, group(z_part, g), ALU.add))
                link(nc.vector.scalar_tensor_tensor(tb, ta, 0.0, ta, ALU.max, ALU.mult))
                root(nc.vector.tensor_reduce(red[:, :], tb, AX.X, ALU.add))
                wait_root()
                link(nc.vector.tensor_scalar(red[:, :], red[:, :], 1e-12, None, ALU.max))
                link(nc.vector.reciprocal(red[:, :], red[:, :]))
                link(nc.vector.scalar_tensor_tensor(tb, ta, 0.0, spread(red[:, :]), ALU.max, ALU.mult))
                link(nc.vector.tensor_tensor(tb, tb, group(x2, g), ALU.add))
                ask_deviation(tb)
                if g:
                    feature_pair(NG + g - 1, pair3, 2 * NG + g)
                norm_group(group(x3, g), tb, x_ready, NG + g + 1)
            feature_pair(2 * NG - 1, pair3, 3 * NG)

            def last_norm(g):
                n = (2 * NG + g) % 2
                dve.wait_ge(root_out, roots[0] - (g + 1 < NG))
                link(nc.vector.reciprocal(rs[:, n, :], sd[:, n, :]))
                nc.vector.scalar_tensor_tensor(shift[:, n, :], moments[:, n, :, 0], -1.0, rs[:, n, :],
                                               ALU.mult, ALU.mult).then_inc(shift_ready, 1)
                for b in range(GB // 2):
                    ins = nc.vector.tensor_scalar(x4[:, g * GB + b, :], [ta, tb][n][:, b, :], moments[:, n, b, 0:1],
                                                  rs[:, n, b:b + 1], ALU.subtract, ALU.mult)
                    if b < GB // 2 - 1:
                        step.done(ins)
                ins.then_inc(out_dve, 1)

            for g in range(NG):
                if g >= 2:
                    dve.wait_ge(out_act, g - 1)
                    dve.wait_ge(out_dve, g - 1)
                h = [ta, tb][(2 * NG + g) % 2]
                link(nc.vector.scalar_tensor_tensor(h, acc(2, g), unscale, group(x3, g), ALU.mult, ALU.add))
                ask_deviation(h)
                if g:
                    last_norm(g - 1)
            last_norm(NG - 1)

        @block.tensor
        def _(pe):
            def features0():
                pe.wait_ge(xw_in_loaded, 32)
                for k in range(KB):
                    ins = nc.tensor.matmul(XW[k // (KB // 2)][:, bass.ts(k % (KB // 2), F)], xT_s[:, bass.ts(k, P)],
                                           w0_s, start=True, stop=True)
                    if k % (KB // 2) == KB // 2 - 1:
                        ins.then_inc(xw_ready, 1)

            def triple(acc, lhs_hi, lhs_lo, rhs_hi, rhs_lo, start, stop, skip=False):
                nc.tensor.matmul(acc, lhs_hi, rhs_hi, start=start, stop=False, skip_group_check=skip)
                nc.tensor.matmul(acc, lhs_hi, rhs_lo, start=False, stop=False, skip_group_check=skip)
                return nc.tensor.matmul(acc, lhs_lo, rhs_hi, start=False, stop=stop, skip_group_check=skip)

            def row_block(r, u):
                for t in range(4):
                    part, h = t // 2, t % 2
                    if h == 0:
                        pe.wait_ge([hi_ready, lo_ready][part], r + 1)
                    if not (isinstance(r, int) and r == 0):
                        pe.wait_ge(tp_evac[t], r)
                    for k in range(KB // 2):
                        ins = nc.tensor.transpose(banks[t][:, :].bitcast(F16)[:, bass.ts(k, P)],
                                                  nat[u][:, part, bass.ts(h * KB // 2 + k, P)], ident16[:, :])
                    ins.then_inc(tp_ready[t], 1)
                    if t == 1:
                        for k in range(KB):
                            nc.tensor.matmul(FLAGS[:, bass.ds(r * KB + k, 1)], nat[u][:, HI, bass.ts(k, P)],
                                             ones16[:, 0:1], start=True, stop=True, skip_group_check=True)

            pe.wait_ge(ident_ready, 1)
            row_block(0, 0)
            row_block(1, 1)
            features0()
            with pe.Fori(1, KB // 2) as pair:
                row_block(pair * 2, 0)
                row_block(pair * 2 + 1, 1)
            nc.tensor.matmul(FLAGS[:, KB * KB:KB * KB + 1], ident16[:, :], ident16[:, 0:1],
                             start=True, stop=True, skip_group_check=True).then_inc(flags_ready, 1)

            def positions():
                pe.wait_ge(tables_ready, 1)
                flags = flags16.rearrange("p (r k) -> p r k", k=KB)
                pos = POS[:, 0:KB * KB].rearrange("p (r k) -> p r k", k=KB)
                nc.tensor.matmul(pos, tri, flags, start=True, stop=False, skip_group_check=True)
                for s in range(1, KB):
                    nc.tensor.matmul(pos[:, :, s:KB], ones16[:, :], flags[:, :, 0:KB - s], start=False,
                                     stop=(s == KB - 1), skip_group_check=True)
                nc.tensor.matmul(COUNTS[:, 0:KB * KB], ones16[:, :], flags16, start=True, stop=True) \
                    .then_inc(pos_ready, 1)

            def list_step(n):
                r, h = n // 2, n % 2
                buf = n % 3
                pe.wait_ge(onehot_dve, n + 1)
                if by_act(n):
                    pe.wait_ge(onehot_act, n // 3 + 1)
                for k in range(HALF):
                    ins = nc.tensor.matmul(LISTS[:, r * KB:r * KB + KB], lower[:, buf, k, :], upper[:, buf, k, :],
                                           start=(h == 0 and k == 0), stop=(h == 1 and k == HALF - 1),
                                           skip_group_check=True)
                ins.then_inc(onehot_used, 1)

            def matvec(n):
                pe.wait_ge(vec_ready, n + 1)
                for i in range(KB):
                    for k in range(KB):
                        nc.tensor.matmul(VEC[:, 2 * i:2 * i + 2], a_block(HI, k, i), vec16[:, k, :],
                                         start=(k == 0), stop=False, skip_group_check=True)
                        nc.tensor.matmul(VEC[:, 2 * i:2 * i + 1], a_block(LO, k, i), vec16[:, k, HI:HI + 1],
                                         start=False, stop=(k == KB - 1), skip_group_check=True)
                    list_step(n * KB + i)
                nc.tensor.matmul(VEC[:, 2 * KB:2 * KB + 1], ident16[:, :], ident16[:, 0:1],
                                 start=True, stop=True).then_inc(mv_ready, 1)

            def spread_g(q):
                pe.wait_ge(gdiag_ready, 2 * q + 2)
                if q:
                    pe.wait_ge(g_ready, q)
                nc.tensor.matmul(VEC[:, :], ones16[:, :], g_diag[:, q, HI].rearrange("p k c -> p (k c)"),
                                 start=True, stop=False)
                nc.tensor.matmul(VEC[:, :], ones16[:, :], g_diag[:, q, LO].rearrange("p k c -> p (k c)"),
                                 start=False, stop=True).then_inc(gbank_ready, 1)

            for t in range(4):
                pe.wait_ge(tp_evac[t], KB)
            positions()
            matvec(0)
            matvec(1)
            def block_products(lhs_hi, lhs_lo, slot, c, start, stop):
                cols = bass.ts(c, CW)
                return triple(banks[c][:, :], lhs_hi, lhs_lo, slots[:, slot, HI, cols], slots[:, slot, LO, cols],
                              start, stop, skip=True)

            more = unit_count(pe)
            units, total = more + 1, more * KB + KB

            def row_of_products(i):
                pe.wait_ge(own_loaded, 16 * i + 16)
                for c in range(CH):
                    pe.wait_ge(tile_evac, units * (i * CH) + (c + 1))
                    ins = block_products(a_block(HI, i, i), a_block(LO, i, i), UNIT, c, True, False)
                ins.then_inc(own_used, 1)
                if i == 0:
                    for q in range(CH):
                        spread_g(q)
                with pe.Fori(0, units) as g:
                    v = units * i + g
                    for b in range(UNIT):
                        pe.wait_ge(r_loaded[b], v * 16 + 16)
                        pe.wait_ge(listed_ready, v * UNIT + (b + 1))
                        for c in range(CH):
                            if b == 0:
                                pe.wait_ge(tile_evac, v * CH + (c + 1))
                            ins = block_products(listed[:, b, HI, :], listed[:, b, LO, :], b, c, False,
                                                 b == UNIT - 1)
                            if b == UNIT - 1:
                                ins.then_inc(tile_ready, 1)
                        if b < UNIT - 1:
                            ins.then_inc(slot_used[b], 1)

            def aggregate(first_bank, pair, ks):
                per = 512 // F
                if ks[-1] < KB - 1:
                    order = [(i, k) for k in ks for i in range(KB)]
                else:
                    order = [(i, k) for i in range(KB) for k in ks]
                for i, k in order:
                    ins = triple(banks[first_bank + i // per][:, bass.ts(i % per, F)], a_block(HI, k, i),
                                 a_block(LO, k, i), pair[:, k, HI, :], pair[:, k, LO, :],
                                 k == 0 and i % per == 0, k == KB - 1, skip=True)
                    if k == KB - 1 and i % per == per - 1:
                        ins.then_inc(acc_ready, 1)

            for i in range(KB + LAG):
                if i < KB:
                    row_of_products(i)
                if i >= LAG:
                    pe.wait_ge(x1_ready, units * (i - LAG + 1))
                    aggregate(4, x1_pair, [i - LAG])

            def project(n, w, width):
                g = n % NG
                src = [x2, x3][n // NG]
                pe.wait_ge(x_ready, n + 1)
                if n >= 2:
                    pe.wait_ge(u_evac, 2 * (n - 1) if n <= NG + 1 else NG + n - 1)
                for b in range(0, GB, 2):
                    ins = nc.tensor.transpose(banks[2 * (n % 2)][:, bass.ts(b // 2, P)],
                                              src[:, g * GB + b:g * GB + b + 2, :].rearrange("p k f -> p (k f)"),
                                              ident[:, :])
                ins.then_inc(xt_ready, 1)
                pe.wait_ge(xt_copied, n + 1)
                for b in range(GB // 2):
                    ins = nc.tensor.matmul(banks[2 * (n % 2) + 1][:, bass.ts(b, 2 * width)],
                                           x_t[n % 2][:, bass.ts(b, P)], w[:, :, :].rearrange("p b f -> p (b f)"),
                                           start=True, stop=True)
                ins.then_inc(u_ready, 1)

            pe.wait_ge(const_loaded, 96)
            for layer, (w, width, pair, first_bank) in enumerate([(w2_s, 2 * F, pair2, 6), (w3_s, F, pair3, 4)]):
                base = layer * NG
                project(base, w, width)
                for g in range(NG):
                    if g + 1 < NG:
                        project(base + g + 1, w, width)
                    pe.wait_ge(pair_ready, base + g + 1)
                    aggregate(first_bank, pair, range(g * GB, g * GB + GB))


def kernel(x, adj, L0_gnn_theta, L0_gnn_W, L0_gnn_b, L1_gnn_t, L2_gnn_W, L2_gnn_b, L3_gnn_weight):
    import numpy as np
    import concourse.bacc as bacc
    from concourse.bass_utils import run_bass_kernel_spmd

    x, adj, w0, w2 = np.asarray(x), np.asarray(adj), np.asarray(L0_gnn_W), np.asarray(L2_gnn_W)
    n, f = x.shape
    kb = n // P
    adjT = np.zeros((kb, n + 1, P), adj.dtype)
    adjT[:, 1:] = adj.reshape(kb, P, n).transpose(0, 2, 1)
    lane, block = np.arange(P), np.arange(kb)
    tables = np.concatenate([
        lane[:, None] < lane[None, :],
        np.broadcast_to(lane, (P, P)),
        np.broadcast_to(np.repeat(block * (n + 1), kb), (P, kb * kb)),
        block[None, :] * P + lane[:, None] + 1,
    ], axis=1).astype(np.float32)
    arrays = {
        "xT": np.ascontiguousarray(x.T),
        "x": x,
        "adj": adj,
        "adjT": adjT.reshape(-1, P),
        "tables": tables,
        "theta": np.asarray(L0_gnn_theta),
        "w0T": np.ascontiguousarray(w0.T),
        "b0": np.asarray(L0_gnn_b),
        "w2": np.ascontiguousarray(np.concatenate([w2[:f], w2[f:]], axis=1)),
        "b2": np.asarray(L2_gnn_b),
        "w3": np.asarray(L3_gnn_weight),
    }
    nc = bacc.Bacc("TRN2", target_bir_lowering=False, num_devices=1)
    args = [nc.dram_tensor(name, a.shape, mybir.dt.from_np(a.dtype), kind="ExternalInput").ap()
            for name, a in arrays.items()]
    xw = nc.dram_tensor("xw", (n, f), F32, kind="Internal").ap()
    r = nc.dram_tensor("r_pairs", (n, 2 * n), F16, kind="Internal").ap()
    out = nc.dram_tensor("out", (n, f), F32, kind="ExternalOutput").ap()
    graph_layers(nc, *args, xw, r, out)
    r = run_bass_kernel_spmd(nc, [arrays], core_ids=[0])
    return r.results[0]["out"]
```

```python
from contextlib import ExitStack

import concourse.bass as bass
from concourse import mybir


ALU = mybir.AluOpType
ACT = mybir.ActivationFunctionType
AX = mybir.AxisListType
F32 = mybir.dt.float32
F16 = mybir.dt.float16
U32 = mybir.dt.uint32

P = 128
A_SCALE = 2.0 ** 12
R_SCALE = 2.0 ** 14
V_SCALE = 2.0 ** 10
EPS = 1e-5
HI, LO = 0, 1


def wait_apart(eng, sem, value):
    if not isinstance(value, int):
        value = eng.to_reg(value)
        eng.wait_ge(sem, 1)
    eng.wait_ge(sem, value)


class Steps:

    def __init__(self, eng, sem):
        self.eng, self.sem, self.base, self.n = eng, sem, 0, 0

    def done(self, ins):
        ins.then_inc(self.sem, 1)
        self.n += 1

    def settle(self):
        self.eng.wait_ge(self.sem, self.base + self.n)

    def link(self, ins):
        self.done(ins)
        self.settle()

    def settle_apart(self):
        wait_apart(self.eng, self.sem, self.base + self.n)

    def link_apart(self, ins):
        self.done(ins)
        self.settle_apart()

    def enter(self, turn, per):
        self.start, self.per = self.base + self.n, per
        self.base, self.n = self.start + turn * per, 0

    def leave(self, turns):
        assert self.n == self.per, self.n
        self.base, self.n = self.start + turns * self.per, 0


def graph_layers(nc, xT, x, adj, adjT, tables, theta, w0T, b0, w2, b2, w3, xw_dram, r_dram, out):
    N, F = x.shape
    KB = N // P
    CW = 512
    CH = N // CW
    DIAG = CW // P
    TOP = 4
    UNIT = 4
    SLOT = (N - P) // KB
    MOST_UNITS = KB // UNIT
    assert SLOT * KB == N - P
    LAG = 2
    GB = 4
    NG = KB // GB
    FAR = 4096.0

    with ExitStack() as ctx:
        def sb(name, shape, dt):
            return ctx.enter_context(nc.sbuf_tensor(name, shape, dt))

        def sem(name):
            return ctx.enter_context(nc.semaphore(name))

        at = sb("at", [P, 2, KB, N], F16)
        slots = sb("slots", [P, UNIT + 1, 2, N], F16)
        row = sb("row", [P, N], F32)
        g_bc = sb("g_bc", [P, N], F32)
        listed_f = sb("listed_f", [P, UNIT, P], F32)
        listed = sb("listed", [P, UNIT, 2, P], F16)
        xb = sb("xb", [P, KB, F], F32)
        x1_mem = sb("x1_mem", [P, 2, KB * F], F32)
        x1 = x1_mem[:, 0, :].rearrange("p (k f) -> p k f", f=F)
        x1_pair = x1_mem[:, 1, :].bitcast(F16).rearrange("p (k u f) -> p k u f", u=2, f=F)
        node16 = sb("node16", [P, KB], F16)
        list_r = sb("list_r", [SLOT, KB * KB], U32)
        list_at = sb("list_at", [SLOT, KB * KB], U32)
        pick_r = sb("pick_r", [SLOT, UNIT], U32)
        pick_at = sb("pick_at", [SLOT, UNIT], U32)
        more_units = sb("more_units", [P, 1], U32)
        gathered = sb("gathered", [P, TOP, F], F32)
        y0 = sb("y0", [P, F], F32)
        ident = sb("ident", [P, P], F32)
        ident16 = sb("ident16", [P, P], F16)
        ones16 = sb("ones16", [P, P], F16)
        w2_s = sb("w2_s", [P, 2, 2 * F], F32)
        w3_s = sb("w3_s", [P, 2, F], F32)
        bias2 = sb("bias2", [P, F], F32)
        th = sb("th", [P, 2], F32)
        t01 = sb("t01", [P, 2], F32)
        t1_scaled = sb("t1_scaled", [P, 1], F32)
        t0_scaled = sb("t0_scaled", [P, 1], F32)
        d_scaled = sb("d_scaled", [P, KB], F32)
        c_row = sb("c_row", [P, KB], F32)
        dinv = sb("dinv", [P, KB], F32)
        droot = sb("droot", [P, KB], F32)
        vec = sb("vec", [P, KB], F32)
        vec16 = sb("vec16", [P, KB, 2], F16)
        mv_s = sb("mv_s", [P, KB, 2], F32)
        u_s = sb("u_s", [P, KB], F32)
        d2 = sb("d2", [P, KB], F32)
        dinv2 = sb("dinv2", [P, KB], F32)
        g_col = sb("g_col", [P, KB], F32)
        g_hi = sb("g_hi", [P, KB], F16)
        g_out = sb("g_out", [P, KB], F32)
        q_col = sb("q_col", [P, KB], F32)
        rdeg = sb("rdeg", [P, KB], F32)
        eps_s = sb("eps_s", [P, 1], F32)
        one_s = sb("one_s", [P, 1], F32)
        best = sb("best", [P, 8], F32)
        next_best = sb("next_best", [P, 8], F32)
        next_idx = sb("next_idx", [P, 8], U32)
        gather_idx = sb("gather_idx", [P, TOP], U32)
        stats = sb("stats", [P, GB, 6], F32)
        moments = sb("moments", [P, 2, GB, 2], F32)
        sd = sb("sd", [P, 2, GB], F32)
        rs = sb("rs", [P, 2, GB], F32)
        shift = sb("shift", [P, 2, GB], F32)
        red = sb("red", [P, GB], F32)

        banks = [ctx.enter_context(nc.psum_tensor(f"bank{i}", [P, 512], F32)) for i in range(8)]
        FLAGS, COUNTS, VEC, POS = banks[5], banks[4], banks[6], banks[7]
        LISTS = [banks[5], banks[4]]
        G_BANKS = [banks[6], banks[7], banks[2], banks[3]]
        EARLY = 10
        XW = [banks[6], banks[7]]

        def flat(t):
            return t.rearrange("p u n -> p (u n)")

        rows = [flat(slots[:, u]).bitcast(F32) for u in range(2)]
        nat = [slots[:, 2 + u] for u in range(2)]
        r_out = [slots[:, UNIT], row[:, :].bitcast(F16).rearrange("p (u n) -> p u n", u=2)]
        xT_s = g_bc[0:F, :]
        t0_diag, own_t = listed_f[:, 2, :], listed_f[:, 3, :]
        tri, iota16 = listed[:, 0, HI, :], listed[:, 0, LO, :]
        w0_s = x1_pair[0:F, 0:2, :, :].rearrange("p a b f -> p (a b f)")[:, 0:2 * F].bitcast(F32)
        bias0 = gathered[:, 1, :]
        xw_s = x1
        gathered_last = g_bc[:, 0:TOP * F].rearrange("p (s f) -> p s f", f=F)
        g_diag = x1_mem[:, :, :].rearrange("p a b -> p (a b)").bitcast(F16) \
            .rearrange("p (q u k c) -> p q u k c", q=CH, u=2, c=P)
        HALF = KB // 2
        NT = P + P + KB * KB + KB
        tables_s = g_bc[:, 0:NT]
        tri_f, iota_f = tables_s[:, 0:P], tables_s[:, P:2 * P]
        base_f, node_f = tables_s[:, 2 * P:2 * P + KB * KB], tables_s[:, 2 * P + KB * KB:NT]
        lower_w, upper_w = 3 * HALF * P // 2, 2 * KB * KB // 2
        lower = row[:, 0:lower_w].bitcast(F16).rearrange("p (h k c) -> p h k c", h=3, c=P)
        upper = row[:, lower_w:lower_w + upper_w].bitcast(F16).rearrange("p (h k c) -> p h k c", h=2, c=KB)
        at_tab = [NT]

        def tab(width):
            at_tab[0] += width
            return g_bc[:, at_tab[0] - width:at_tab[0]]

        flags16 = tab(KB * KB // 2).bitcast(F16)
        pos_f = tab(KB * KB)
        upper16 = tab(KB * KB // 2).bitcast(F16)
        lower16 = tab(KB * KB // 2).bitcast(F16)
        number_f = tab(KB * KB)
        assert at_tab[0] <= N
        place_f = listed_f[:, 0:2, :].rearrange("p b c -> p (b c)")

        end = slots[:, :, :, :].rearrange("p a b c -> p (a b c)").bitcast(F32)
        at_end = [0]

        def carve(width):
            at_end[0] += width
            return end[:, at_end[0] - width:at_end[0]]

        def carve_nodes():
            return carve(KB * F).rearrange("p (k f) -> p k f", f=F)

        x2, x3, x1_part = carve_nodes(), carve_nodes(), carve_nodes()
        u_top, u_bot, z_part = carve_nodes(), carve_nodes(), carve_nodes()
        pair2 = carve(KB * F).bitcast(F16).rearrange("p (k u f) -> p k u f", u=2, f=F)
        pair3 = carve(KB * F).bitcast(F16).rearrange("p (k u f) -> p k u f", u=2, f=F)
        ta = carve(GB * F).rearrange("p (k f) -> p k f", f=F)
        tb = carve(GB * F).rearrange("p (k f) -> p k f", f=F)
        x_t = [carve(GB * F) for _ in range(2)]
        x4 = carve_nodes()

        const_loaded = sem("const_loaded")
        xw_in_loaded = sem("xw_in_loaded")
        xb_loaded = sem("xb_loaded")
        rows_loaded = [sem("rows_loaded0"), sem("rows_loaded1")]
        tables_loaded = sem("tables_loaded")
        tables_ready = sem("tables_ready")
        w_zeroed = sem("w_zeroed")
        xw_ready = sem("xw_ready")
        xw_copied = sem("xw_copied")
        xw_stored = sem("xw_stored")
        pool_step = sem("pool_step")
        ident_ready = sem("ident_ready")
        exp_done = sem("exp_done")
        t_ready = sem("t_ready")
        hi_ready = sem("hi_ready")
        lo_ready = sem("lo_ready")
        c_ready = sem("c_ready")
        rhi_ready = sem("rhi_ready")
        r_ready = sem("r_ready")
        r_stored = [sem("r_stored0"), sem("r_stored1")]
        tp_ready = [sem(f"tp_ready{t}") for t in range(4)]
        tp_evac = [sem(f"tp_evac{t}") for t in range(4)]
        flags_ready = sem("flags_ready")
        pos_ready = sem("pos_ready")
        tables_copied = sem("tables_copied")
        places_ready = sem("places_ready")
        onehot_dve = sem("onehot_dve")
        onehot_act = sem("onehot_act")
        upper_ready = sem("upper_ready")
        act_step = sem("act_step")
        onehot_used = sem("onehot_used")
        units_ready = sem("units_ready")
        lists_ready = sem("lists_ready")
        r_loaded = [sem(f"r_loaded{b}") for b in range(UNIT)]
        listed_loaded = [sem(f"listed_loaded{b}") for b in range(UNIT)]
        listed_hi = sem("listed_hi")
        listed_ready = sem("listed_ready")
        slot_used = [sem(f"slot_used{b}") for b in range(UNIT - 1)]
        own_loaded = sem("own_loaded")
        own_used = sem("own_used")
        tile_ready = sem("tile_ready")
        tile_evac = sem("tile_evac")
        row_used = sem("row_used")
        moments_ready = sem("moments_ready")
        sd_ready = sem("sd_ready")
        root_in = sem("root_in")
        root_out = sem("root_out")
        vec_ready = sem("vec_ready")
        mv_ready = sem("mv_ready")
        g_split = sem("g_split")
        gdiag_hi = sem("gdiag_hi")
        gdiag_lo = sem("gdiag_lo")
        gbank_ready = sem("gbank_ready")
        g_ready = sem("g_ready")
        idx_ready = sem("idx_ready")
        rows_gathered = sem("rows_gathered")
        last_gathered = sem("last_gathered")
        x1_ready = sem("x1_ready")
        acc_ready = sem("acc_ready")
        x_ready = sem("x_ready")
        xt_ready = sem("xt_ready")
        xt_copied = sem("xt_copied")
        u_ready = sem("u_ready")
        u_evac = sem("u_evac")
        pair_ready = sem("pair_ready")
        shift_ready = sem("shift_ready")
        out_dve = sem("out_dve")
        out_act = sem("out_act")
        out_stored = sem("out_stored")
        dve_step = sem("dve_step")
        late_step = sem("late_step")

        def a_block(part, k, i):
            return at[:, part, k, bass.ts(i, P)]

        def row_block_of(v, units):
            i = v // units
            return i if isinstance(i, int) else i.with_bounds(min_val=0, max_val=KB - 1)

        def by_act(n):
            return n % 4 == 1

        def unit_count(eng):
            eng.wait_ge(units_ready, 1)
            return eng.value_load(more_units[0:1, 0:1], min_val=0, max_val=MOST_UNITS - 1)

        block = ctx.enter_context(nc.Block())

        @block.sync
        def _(sp):
            sp.dma_start(rows[0], adj[0:P, :]).then_inc(rows_loaded[0], 16)
            sp.dma_start(th[:, :], theta.partition_broadcast(P)).then_inc(const_loaded, 16)
            sp.dma_start(rows[1], adj[P:2 * P, :]).then_inc(rows_loaded[1], 16)
            sp.dma_start(xT_s, xT).then_inc(xw_in_loaded, 16)
            sp.dma_start(w0_s, w0T).then_inc(xw_in_loaded, 16)
            sp.dma_start(xb[:, :, :], x.rearrange("(k p) f -> p k f", p=P)).then_inc(xb_loaded, 16)
            sp.dma_start(bias0, b0.partition_broadcast(P)).then_inc(xb_loaded, 16)

            def row_block(r, u, following=True):
                sp.wait_ge(r_ready, r + 1)
                if following:
                    sp.dma_start(rows[u], adj[bass.ds((r + 2) * P, P), :]).then_inc(rows_loaded[u], 16)
                sp.dma_start(r_dram[bass.ds(r * P, P), :], r_out[u].rearrange("p u n -> p (u n)")) \
                    .then_inc(r_stored[u], 16)

            row_block(0, 0)
            row_block(1, 1)
            sp.wait_ge(xw_copied, 2)
            sp.dma_start(xw_dram.rearrange("(k p) f -> p k f", p=P), xw_s).then_inc(xw_stored, 16)
            sp.dma_start(tables_s, tables).then_inc(tables_loaded, 16)
            sp.dma_start(bias2[:, :], b2.partition_broadcast(P)).then_inc(const_loaded, 16)
            sp.wait_ge(w_zeroed, 2)
            for half in range(2):
                sp.dma_start(w2_s[half * F:half * F + F, half, :], w2).then_inc(const_loaded, 16)
                sp.dma_start(w3_s[half * F:half * F + F, half, :], w3).then_inc(const_loaded, 16)
            with sp.Fori(1, KB // 2 - 1) as pair:
                row_block(pair * 2, 0)
                row_block(pair * 2 + 1, 1)
            row_block(KB - 2, 0, following=False)
            row_block(KB - 1, 1, following=False)
            sp.wait_ge(r_stored[0], 16 * KB // 2)
            sp.wait_ge(r_stored[1], 16 * KB // 2)
            own = slots[:, UNIT].rearrange("p u n -> p (u n)")
            sp.dma_start(own, r_dram[0:P, :]).then_inc(own_loaded, 16)
            with sp.Fori(1, KB) as i:
                sp.wait_ge(own_used, i)
                sp.dma_start(own, r_dram[bass.ds(i * P, P), :]).then_inc(own_loaded, 16)
            out_v = out.rearrange("(k p) f -> p k f", p=P)
            for g in range(NG):
                sp.wait_ge(out_dve, g + 1)
                sp.wait_ge(out_act, g + 1)
                sp.dma_start(out_v[:, g * GB:g * GB + GB, :], x4[:, g * GB:g * GB + GB, :]).then_inc(out_stored, 16)
            sp.wait_ge(out_stored, 16 * NG)

        @block.gpsimd
        def _(pool):
            nc.gpsimd.memset(ones16[:, :], 1.0).then_inc(pool_step, 1)
            pool.wait_ge(pool_step, 1)
            nc.gpsimd.affine_select(out=ident[:, :], in_=ones16[:, :], compare_op=ALU.is_equal, fill=0.0, base=0,
                                    pattern=[[-1, P]], channel_multiplier=1).then_inc(pool_step, 1)
            pool.wait_ge(pool_step, 2)
            nc.gpsimd.tensor_copy(ident16[:, :], ident[:, :]).then_inc(ident_ready, 1)
            nc.gpsimd.memset(w2_s[:, :, :], 0.0).then_inc(w_zeroed, 1)
            nc.gpsimd.memset(w3_s[:, :, :], 0.0).then_inc(w_zeroed, 1)

            pool.wait_ge(tables_loaded, 16)
            nc.gpsimd.tensor_copy(tri, tri_f).then_inc(tables_copied, 1)
            nc.gpsimd.tensor_copy(iota16, iota_f).then_inc(tables_copied, 1)
            nc.gpsimd.tensor_copy(node16[:, :], node_f).then_inc(tables_copied, 1)

            more = unit_count(pool)
            units, total = more + 1, more * KB + KB

            def gather_unit(v):
                first = isinstance(v, int) and v == 0
                slot0 = row_block_of(v, units) * KB + (v % units) * UNIT
                for b in range(UNIT):
                    if not first:
                        pool.wait_ge(listed_ready, v * UNIT + (b + 1 - UNIT))
                    nc.gpsimd.tensor_copy(pick_at[:, b:b + 1], list_at[:, bass.ds(slot0 + b, 1)]) \
                        .then_inc(pool_step, 1)
                    wait_apart(pool, pool_step, v * (2 * UNIT) + (2 * b + 3))
                    pool.indirect_dma_start(
                        out=listed_f[0:SLOT, b, :], out_offset=None, in_=adjT,
                        in_offset=bass.IndirectOffsetOnAxis(ap=pick_at[:, b:b + 1], axis=0),
                    ).then_inc(listed_loaded[b], 16)
                    if not first:
                        if b < UNIT - 1:
                            pool.wait_ge(slot_used[b], v)
                        else:
                            pool.wait_ge(tile_ready, v * CH)
                    nc.gpsimd.tensor_copy(pick_r[:, b:b + 1], list_r[:, bass.ds(slot0 + b, 1)]) \
                        .then_inc(pool_step, 1)
                    wait_apart(pool, pool_step, v * (2 * UNIT) + (2 * b + 4))
                    pool.indirect_dma_start(
                        out=slots[0:SLOT, b].rearrange("p u n -> p (u n)"), out_offset=None, in_=r_dram,
                        in_offset=bass.IndirectOffsetOnAxis(ap=pick_r[:, b:b + 1], axis=0),
                    ).then_inc(r_loaded[b], 16)

            def gather_best(v, last=False):
                if last:
                    wait_apart(pool, row_used, v + 1)
                else:
                    wait_apart(pool, idx_ready, v + 1)
                into, idx = (gathered_last, next_idx) if last else (gathered[:, :, :], gather_idx)
                for s in range(TOP):
                    pool.indirect_dma_start(
                        out=into[:, s, :], out_offset=None, in_=xw_dram,
                        in_offset=bass.IndirectOffsetOnAxis(ap=idx[:, s:s + 1], axis=0),
                    ).then_inc(last_gathered if last else rows_gathered, 16)

            pool.wait_ge(lists_ready, 1)
            pool.wait_ge(xw_stored, 16)
            for u in range(2):
                pool.wait_ge(r_stored[u], 16 * KB // 2)
            pool.wait_ge(tp_ready[3], KB)
            gather_unit(0)
            pool.wait_ge(lists_ready, 2)
            gather_unit(1)
            with pool.Fori(2, total) as v:
                gather_unit(v)
                gather_best(v - 2)
            gather_best(more * KB + (KB - 2))
            gather_best(more * KB + (KB - 1), last=True)

        @block.scalar
        def _(act):
            act.wait_ge(const_loaded, 16)
            nc.scalar.activation(t01[:, :], th[:, :], ACT.Exp, scale=-1.0).then_inc(exp_done, 1)

            def split_hi(r, u, turn):
                act.wait_ge(rows_loaded[u], 16 * turn + 16)
                if not (isinstance(r, int) and r < 2):
                    act.wait_ge(tp_ready[3], r - 1)
                nc.scalar.activation(nat[u][:, HI, :], rows[u], ACT.Copy, scale=A_SCALE,
                                     accum_out=d_scaled[:, bass.ds(r, 1)]).then_inc(hi_ready, 1)

            def row_block(r, u, turn, following=True):
                act.wait_ge(c_ready, r + 1)
                if not (isinstance(r, int) and r < 2):
                    act.wait_ge(r_stored[u], 16 * turn)
                nc.scalar.activation(r_out[u][:, HI, :], rows[u], ACT.Copy, scale=c_row[:, bass.ds(r, 1)]) \
                    .then_inc(rhi_ready, 1)
                evacuate(r, 0)
                if following:
                    split_hi(r + 1, 1 - u, turn + u)
                evacuate(r, 2)
                evacuate(r, 3)

            def evacuate(r, t):
                act.wait_ge(tp_ready[t], r + 1)
                half = t % 2 * KB // 2
                nc.scalar.copy(at[:, t // 2, half:half + KB // 2, bass.ds(r * P, P)],
                               banks[t][:, :].bitcast(F16).rearrange("p (k c) -> p k c", c=P)).then_inc(tp_evac[t], 1)

            split_hi(0, 0, 0)
            row_block(0, 0, 0)
            row_block(1, 1, 0)
            for h in range(2):
                act.wait_ge(xw_ready, h + 1)
                nc.scalar.copy(xw_s[:, h * KB // 2:(h + 1) * KB // 2, :],
                               XW[h][:, :].rearrange("p (k f) -> p k f", f=F)).then_inc(xw_copied, 1)
            with act.Fori(1, KB // 2 - 1) as pair:
                row_block(pair * 2, 0, pair)
                row_block(pair * 2 + 1, 1, pair)
            row_block(KB - 2, 0, KB // 2 - 1)
            row_block(KB - 1, 1, KB // 2 - 1, following=False)

            act.wait_ge(root_in, 1)
            nc.scalar.activation(droot[:, :], u_s[:, :], ACT.Sqrt).then_inc(root_out, 1)
            more = unit_count(act)
            units, total = more + 1, more * KB + KB

            act.wait_ge(places_ready, 1)
            act_steps = 0
            for n in range(2 * KB):
                if n == KB + EARLY:
                    act.wait_ge(root_in, 2)
                    nc.scalar.activation(dinv2[:, :], d2[:, :], ACT.Sqrt).then_inc(root_out, 1)
                    act.wait_ge(g_split, 1)
                    act.wait_ge(xw_stored, 16)
                    for k in range(KB):
                        nc.scalar.activation(g_diag[:, k // DIAG, LO, k % DIAG, :], ident[:, :], ACT.Copy,
                                             scale=u_s[:, k:k + 1]).then_inc(gdiag_lo, 1)
                if by_act(n):
                    if n >= 3:
                        act.wait_ge(onehot_used, n - 2)
                    for k in range(HALF):
                        nc.scalar.activation(lower[:, n % 3, k, :], iota16, ACT.Square,
                                             bias=pos_f[:, n * HALF + k:n * HALF + k + 1]).then_inc(act_step, 1)
                    act_steps += HALF
                    act.wait_ge(act_step, act_steps)
                    nc.scalar.activation(lower[:, n % 3], lower[:, n % 3], ACT.Relu, bias=one_s[:, 0:1], scale=-1.0) \
                        .then_inc(onehot_act, 1)

            def split_listed(v, b):
                if not (isinstance(v, int) and v == 0):
                    if b < UNIT - 1:
                        act.wait_ge(slot_used[b], v)
                    else:
                        act.wait_ge(tile_ready, v * CH)
                act.wait_ge(listed_loaded[b], v * 16 + 16)
                nc.scalar.activation(listed[0:SLOT, b, HI, :], listed_f[0:SLOT, b, :], ACT.Copy, scale=A_SCALE) \
                    .then_inc(listed_hi, 1)

            def evacuate_row(v):
                if not (isinstance(v, int) and v == 0):
                    act.wait_ge(row_used, v)
                for c in range(CH):
                    act.wait_ge(tile_ready, v * CH + (c + 1))
                    nc.scalar.copy(row[:, bass.ts(c, CW)], banks[c][:, :]).then_inc(tile_evac, 1)

            def unit(v, after_first=True):
                for b in range(UNIT - 1):
                    split_listed(v + 1, b)
                evacuate_row(v)
                split_listed(v + 1, UNIT - 1)
                if after_first:
                    deviation0(v - 1)

            def deviation0(v):
                act.wait_ge(moments_ready, v + 1)
                nc.scalar.activation(sd[:, 0, 0:1], moments[:, 0, 0, 1:2], ACT.Sqrt, bias=eps_s[:, 0:1]) \
                    .then_inc(sd_ready, 1)

            for b in range(UNIT):
                split_listed(0, b)
            act.wait_ge(lists_ready, 2)
            act.wait_ge(gbank_ready, CH)
            for q in (2, 3, 0, 1):
                nc.scalar.mul(g_bc[:, bass.ts(q, CW)], G_BANKS[q][:, :], 1.0 / V_SCALE).then_inc(g_ready, 1)
                if q == 3:
                    act.wait_ge(g_ready, 2)
                    nc.scalar.copy(sd[:, 1, 0:1], eps_s[:, 0:1]).then_inc(tile_evac, CH)
            unit(0, after_first=False)
            with act.Fori(1, more * KB + (KB - 1)) as v:
                unit(v)
            deviation0(more * KB + (KB - 2))
            deviation0(more * KB + (KB - 1))

            roots = [2]

            def root(out_ap, in_ap, bias_ap=0.0):
                roots[0] += 1
                act.wait_ge(root_in, roots[0])
                nc.scalar.activation(out_ap, in_ap, ACT.Sqrt, bias=bias_ap).then_inc(root_out, 1)

            def deviation(n):
                root(sd[:, n % 2, :], moments[:, n % 2, :, 1], eps_s[:, 0:1])

            def turn_features(n):
                act.wait_ge(xt_ready, n + 1)
                nc.scalar.copy(x_t[n % 2], banks[2 * (n % 2)][:, 0:GB * F]).then_inc(xt_copied, 1)

            def evacuate_features(n, parts):
                act.wait_ge(u_ready, n + 1)
                g, width = n % NG, F * len(parts)
                u = banks[2 * (n % 2) + 1][:, 0:GB * width].rearrange("p (k f) -> p k f", f=width)
                for at_f, dst in parts:
                    nc.scalar.copy(dst[:, g * GB:g * GB + GB, :], u[:, :, at_f:at_f + F]).then_inc(u_evac, 1)

            deviation(0)
            for g in range(NG):
                turn_features(g)
                if g + 1 < NG:
                    deviation(g + 1)
                evacuate_features(g, [(F, u_bot), (0, u_top)])
            for g in range(NG):
                root(red[:, :], red[:, :])
                deviation(NG + g)
                if g:
                    evacuate_features(NG + g - 1, [(0, u_bot)])
                turn_features(NG + g)
            evacuate_features(2 * NG - 1, [(0, u_bot)])

            def last_norm(g):
                act.wait_ge(shift_ready, g + 1)
                n = (2 * NG + g) % 2
                for b in range(GB // 2, GB):
                    ins = nc.scalar.activation(x4[:, g * GB + b, :], [ta, tb][n][:, b, :], ACT.Identity,
                                               bias=shift[:, n, b:b + 1], scale=rs[:, n, b:b + 1])
                ins.then_inc(out_act, 1)

            deviation(2 * NG)
            for g in range(NG):
                if g + 1 < NG:
                    deviation(2 * NG + g + 1)
                last_norm(g)

        @block.vector
        def _(dve):
            step = Steps(dve, dve_step)
            link = step.link
            roots = [0]

            def row_block(r, u, turn):
                late = not (isinstance(r, int) and r < 2)
                dve.wait_ge(hi_ready, r + 1)
                scale = c_row[:, bass.ds(r, 1)]
                link(nc.vector.reciprocal(scale, d_scaled[:, bass.ds(r, 1)]))
                nc.vector.tensor_scalar(scale, scale, t1_scaled[:, 0:1], None, ALU.mult).then_inc(c_ready, 1)
                own = bass.ds(r * P, P)
                dve.wait_ge(c_ready, r + 1)
                step.done(nc.vector.scalar_tensor_tensor(own_t, rows[u][:, own], scale, t0_diag,
                                                         ALU.mult, ALU.add))
                nc.vector.scalar_tensor_tensor(nat[u][:, LO, :], rows[u], A_SCALE, nat[u][:, HI, :],
                                               ALU.mult, ALU.subtract).then_inc(lo_ready, 1)
                evacuate(r, 1)
                dve.wait_ge(rhi_ready, r + 1)
                link(nc.vector.scalar_tensor_tensor(r_out[u][:, LO, :], rows[u], scale, r_out[u][:, HI, :],
                                                         ALU.mult, ALU.subtract))
                link(nc.vector.tensor_copy(r_out[u][:, HI, own], own_t))
                nc.vector.tensor_tensor(r_out[u][:, LO, own], own_t, r_out[u][:, HI, own],
                                        ALU.subtract).then_inc(r_ready, 1)
                dve.wait_ge(r_ready, r + 1)

            def evacuate(r, t):
                dve.wait_ge(tp_ready[t], r + 1)
                nc.vector.tensor_copy(at[:, t // 2, KB // 2:KB, bass.ds(r * P, P)],
                                      banks[t][:, :].bitcast(F16).rearrange("p (k c) -> p k c", c=P)) \
                    .then_inc(tp_evac[t], 1)

            nc.vector.memset(eps_s[:, :], EPS)
            nc.vector.memset(one_s[:, :], 1.0)
            dve.wait_ge(exp_done, 1)
            link(nc.vector.tensor_scalar(t01[:, :], t01[:, :], 1.0, None, ALU.add))
            link(nc.vector.reciprocal(t01[:, :], t01[:, :]))
            link(nc.vector.tensor_scalar(t1_scaled[:, :], t01[:, 1:2], A_SCALE * R_SCALE, None, ALU.mult))
            link(nc.vector.tensor_scalar(t0_scaled[:, :], t01[:, 0:1], R_SCALE, None, ALU.mult))
            dve.wait_ge(ident_ready, 1)
            link(nc.vector.tensor_scalar(t0_diag, ident[:, :], t0_scaled[:, 0:1], None, ALU.mult))

            row_block(0, 0, 0)
            row_block(1, 1, 0)
            with dve.Fori(1, KB // 2) as pair:
                step.enter(pair - 1, 8)
                row_block(pair * 2, 0, pair)
                row_block(pair * 2 + 1, 1, pair)
                step.leave(KB // 2 - 1)

            def root(value):
                value.then_inc(root_in, 1)
                roots[0] += 1

            def wait_root():
                dve.wait_ge(root_out, roots[0])

            def split_vec():
                link(nc.vector.tensor_scalar(vec[:, :], vec[:, :], V_SCALE, None, ALU.mult))
                link(nc.vector.tensor_copy(vec16[:, :, HI], vec[:, :]))
                nc.vector.tensor_tensor(vec16[:, :, LO], vec[:, :], vec16[:, :, HI], ALU.subtract) \
                    .then_inc(vec_ready, 1)

            def matvec_out(n):
                dve.wait_ge(mv_ready, n + 1)
                link(nc.vector.tensor_copy(mv_s[:, :, :], VEC[:, 0:2 * KB].rearrange("p (k t) -> p k t", t=2)))
                link(nc.vector.tensor_tensor(vec[:, :], mv_s[:, :, 0], mv_s[:, :, 1], ALU.add))
                link(nc.vector.tensor_scalar(vec[:, :], vec[:, :], 1.0 / (A_SCALE * V_SCALE), None, ALU.mult))

            root(nc.vector.tensor_scalar(u_s[:, :], d_scaled[:, :], 1.0 / A_SCALE, None, ALU.mult))
            dve.wait_ge(root_in, 1)
            link(nc.vector.tensor_scalar(rdeg[:, :], u_s[:, :], 1.0, 1.0, ALU.add, ALU.max))
            link(nc.vector.reciprocal(rdeg[:, :], rdeg[:, :]))
            wait_root()
            link(nc.vector.reciprocal(dinv[:, :], droot[:, :]))
            link(nc.vector.tensor_copy(vec[:, :], dinv[:, :]))
            split_vec()

            dve.wait_ge(tables_copied, 3)
            dve.wait_ge(flags_ready, 1)
            link(nc.vector.tensor_scalar(flags16, FLAGS[:, 0:KB * KB], 0.0, None, ALU.is_gt))
            step.done(nc.vector.memset(flags16[:, 0:KB * KB:KB + 1], 0.0))
            step.settle()
            nc.vector.tensor_scalar(pos_f, flags16, -FAR, FAR, ALU.mult, ALU.add).then_inc(tables_ready, 1)
            dve.wait_ge(tables_ready, 1)
            dve.wait_ge(pos_ready, 1)
            link(nc.vector.tensor_tensor(pos_f, pos_f, POS[:, 0:KB * KB], ALU.add))
            link(nc.vector.tensor_reduce(u_s[:, :], COUNTS[:, 0:KB * KB].rearrange("p (r k) -> p r k", k=KB),
                                         AX.X, ALU.add))
            link(nc.vector.tensor_reduce(red[:, 0:1], u_s[:, :], AX.X, ALU.max))
            link(nc.vector.tensor_scalar(red[:, 1:2], red[:, 0:1], float(UNIT * SLOT), None, ALU.is_gt))
            for n in range(2, MOST_UNITS):
                link(nc.vector.tensor_scalar(red[:, 2:3], red[:, 0:1], float(UNIT * SLOT * n), None, ALU.is_gt))
                link(nc.vector.tensor_tensor(red[:, 1:2], red[:, 1:2], red[:, 2:3], ALU.add))
            nc.vector.tensor_copy(more_units[:, :], red[:, 1:2]).then_inc(units_ready, 1)
            link(nc.vector.tensor_scalar(place_f, pos_f, 1.0 / SLOT, -0.498, ALU.mult, ALU.add))
            link(nc.vector.tensor_scalar(place_f, place_f, 1.5 * 2.0 ** 23, None, ALU.add))
            link(nc.vector.tensor_scalar(place_f, place_f, -1.5 * 2.0 ** 23, None, ALU.add))
            link(nc.vector.scalar_tensor_tensor(lower16, place_f, -float(SLOT), pos_f, ALU.mult, ALU.add))

            def evacuate_lists(half):
                dve.wait_ge(onehot_used, KB * (half + 1))
                cols = slice(half * KB * HALF, (half + 1) * KB * HALF)
                lists = LISTS[half][0:SLOT, 0:KB * HALF]
                link(nc.vector.tensor_scalar(number_f[0:SLOT, cols], lists, 0.0, node_f[0:SLOT, 0:1],
                                             ALU.is_equal, ALU.mult))
                link(nc.vector.tensor_tensor(number_f[0:SLOT, cols], number_f[0:SLOT, cols], lists, ALU.add))
                link(nc.vector.tensor_scalar(list_r[:, cols], number_f[0:SLOT, cols], -1.0, None, ALU.add))
                nc.vector.tensor_tensor(list_at[:, cols], lists, base_f[0:SLOT, cols], ALU.add) \
                    .then_inc(lists_ready, 1)

            def onehots(n):
                h, buf, cols = n % 2, n % 3, slice(n * HALF, n * HALF + HALF)
                if n >= 3:
                    dve.wait_ge(onehot_used, n - 2)
                if h == 0:
                    both = slice(n * HALF, (n + 2) * HALF)
                    link(nc.vector.tensor_tensor(upper[:, n // 2 % 2],
                                                 iota16[:, 0:KB].unsqueeze(1).to_broadcast([P, KB, KB]),
                                                 upper16[:, both].unsqueeze(2).to_broadcast([P, KB, KB]),
                                                 ALU.is_equal))
                    nc.vector.tensor_tensor(upper[:, n // 2 % 2], upper[:, n // 2 % 2],
                                            node16[:, :].unsqueeze(2).to_broadcast([P, KB, KB]),
                                            ALU.mult).then_inc(upper_ready, 1)
                if not by_act(n):
                    nc.vector.tensor_tensor(lower[:, buf], iota16.unsqueeze(1).to_broadcast([P, HALF, P]),
                                            lower16[:, cols].unsqueeze(2).to_broadcast([P, HALF, P]),
                                            ALU.is_equal).then_inc(onehot_dve, 1)

            dve.wait_ge(r_stored[1], 16 * KB // 2)
            link(nc.vector.tensor_copy(upper16, place_f))
            nc.vector.tensor_scalar(pos_f, lower16, -1.0, None, ALU.mult).then_inc(places_ready, 1)
            for n in range(EARLY):
                onehots(n)
            matvec_out(0)
            link(nc.vector.tensor_tensor(u_s[:, :], vec[:, :], dinv[:, :], ALU.mult))
            link(nc.vector.tensor_tensor(vec[:, :], u_s[:, :], dinv[:, :], ALU.mult))
            split_vec()
            for n in range(EARLY, KB + EARLY):
                onehots(n)
                if n == KB + 2:
                    evacuate_lists(0)
            matvec_out(1)
            link(nc.vector.tensor_tensor(vec[:, :], vec[:, :], dinv[:, :], ALU.mult))
            link(nc.vector.tensor_scalar(d2[:, :], u_s[:, :], t01[:, 0:1], 1.0, ALU.mult, ALU.add))
            root(nc.vector.scalar_tensor_tensor(d2[:, :], vec[:, :], t01[:, 1:2], d2[:, :], ALU.mult, ALU.add))
            wait_root()
            link(nc.vector.reciprocal(dinv2[:, :], dinv2[:, :]))
            link(nc.vector.tensor_tensor(g_col[:, :], dinv[:, :], dinv2[:, :], ALU.mult))
            step.done(nc.vector.tensor_scalar(g_out[:, :], g_col[:, :], 1.0 / (A_SCALE * R_SCALE), None, ALU.mult))
            link(nc.vector.scalar_tensor_tensor(q_col[:, :], dinv2[:, :], A_SCALE * R_SCALE, droot[:, :],
                                                ALU.mult, ALU.mult))
            link(nc.vector.tensor_scalar(vec[:, :], g_col[:, :], V_SCALE, None, ALU.mult))
            link(nc.vector.tensor_copy(g_hi[:, :], vec[:, :]))
            nc.vector.tensor_tensor(u_s[:, :], vec[:, :], g_hi[:, :], ALU.subtract).then_inc(g_split, 1)

            def spread_g(q):
                blocks = slice(q * DIAG, q * DIAG + DIAG)
                nc.vector.tensor_tensor(g_diag[:, q, HI], ident[:, :].unsqueeze(1).to_broadcast([P, DIAG, P]),
                                        vec[:, blocks].unsqueeze(2).to_broadcast([P, DIAG, P]),
                                        ALU.mult).then_inc(gdiag_hi, 1)

            def split_listed(v, b):
                dve.wait_ge(listed_hi, v * UNIT + (b + 1))
                nc.vector.scalar_tensor_tensor(listed[0:SLOT, b, LO, :], listed_f[0:SLOT, b, :], A_SCALE,
                                               listed[0:SLOT, b, HI, :], ALU.mult, ALU.subtract).then_inc(listed_ready, 1)

            dve.wait_ge(xw_stored, 16)
            for q in range(CH):
                spread_g(q)
            for n in range(KB + EARLY, 2 * KB):
                onehots(n)
            evacuate_lists(1)
            for b in range(UNIT):
                split_listed(0, b)
            dve.wait_ge(xb_loaded, 32)
            link(nc.vector.tensor_tensor(xb[:, :, :], xb[:, :, :],
                                         bias0.unsqueeze(1).to_broadcast([P, KB, F]), ALU.add))

            def measure(n, h):
                for b in range(len(h)):
                    step.done(nc.vector.bn_stats(stats[:, b, :], h[b]))
                step.settle_apart()
                for b in range(len(h)):
                    ins = nc.vector.bn_aggr(moments[:, n, b, :], stats[:, b, :])
                    if b < len(h) - 1:
                        step.done(ins)
                return ins

            more = unit_count(dve)
            units, total = more + 1, more * KB + KB

            def scale_row(v):
                i = row_block_of(v, units)
                dve.wait_ge(tile_evac, v * CH + 2 * CH)
                link(nc.vector.tensor_tensor(row[:, :], row[:, :], g_bc[:, :], ALU.mult))
                own = bass.ds(i * P, P)
                step.done(nc.vector.scalar_tensor_tensor(row[:, own], ident[:, :], q_col[:, bass.ds(i, 1)],
                                                         row[:, own], ALU.mult, ALU.add))

            def select(v):
                step.link_apart(nc.vector.max(next_best[:, :], row[:, :]))
                nc.vector.max_index(next_idx[:, :], next_best[:, :], row[:, :]).then_inc(row_used, 1)

            def hand_over(v):
                dve.wait_ge(row_used, v + 1)
                step.done(nc.vector.tensor_copy(best[:, :], next_best[:, :]))
                nc.vector.tensor_copy(gather_idx[:, :], next_idx[:, 0:TOP]).then_inc(idx_ready, 1)

            def finish(v, rows=gathered[:, :, :], weights=best):
                i = row_block_of(v, units)
                h0 = rows[:, 0, :]
                if weights is best:
                    dve.wait_ge(rows_gathered, v * (16 * TOP) + 16 * TOP)
                else:
                    dve.wait_ge(last_gathered, 16 * TOP)
                step.settle()
                link(nc.vector.tensor_tensor(rows, rows, weights[:, 0:TOP].unsqueeze(2).to_broadcast([P, TOP, F]),
                                             ALU.mult))
                link(nc.vector.tensor_reduce(y0[:, :], rows.rearrange("p s f -> p f s"), AX.X, ALU.add))
                link(nc.vector.scalar_tensor_tensor(h0, y0[:, :], g_out[:, bass.ds(i, 1)],
                                                    xb[:, bass.ds(i, 1), :].squeeze(1), ALU.mult, ALU.add))
                measure(0, [h0]).then_inc(moments_ready, 1)
                dve.wait_ge(sd_ready, v + 1)
                link(nc.vector.reciprocal(rs[:, 0, 0:1], sd[:, 0, 0:1]))
                link(nc.vector.tensor_scalar(x1[:, bass.ds(i, 1), :].squeeze(1), h0, moments[:, 0, 0, 0:1],
                                             rs[:, 0, 0:1], ALU.subtract, ALU.mult))
                link(nc.vector.tensor_scalar(x1_pair[:, bass.ds(i, 1), HI, :].squeeze(1),
                                             x1[:, bass.ds(i, 1), :].squeeze(1), V_SCALE, None, ALU.mult))
                nc.vector.scalar_tensor_tensor(x1_pair[:, bass.ds(i, 1), LO, :].squeeze(1),
                                               x1[:, bass.ds(i, 1), :].squeeze(1), V_SCALE,
                                               x1_pair[:, bass.ds(i, 1), HI, :].squeeze(1),
                                               ALU.mult, ALU.subtract).then_inc(x1_ready, 1)

            def unit(v, after_first=True):
                for b in range(UNIT - 1):
                    split_listed(v + 1, b)
                scale_row(v)
                split_listed(v + 1, UNIT - 1)
                step.settle_apart()
                select(v)
                if after_first:
                    finish(v - 1)
                hand_over(v)

            dve.wait_ge(g_ready, CH)
            unit(0, after_first=False)
            with dve.Fori(1, more * KB + (KB - 1)) as v:
                step.enter(v - 1, 11)
                unit(v)
                step.leave(more * KB + (KB - 2))
            for c in range(CH):
                dve.wait_ge(tile_ready, total * CH - (CH - 1 - c))
                step.done(nc.vector.tensor_tensor(row[:, bass.ts(c, CW)], banks[c][:, :], g_bc[:, bass.ts(c, CW)],
                                                  ALU.mult))
            step.settle()
            own = bass.ts(KB - 1, P)
            step.done(nc.vector.scalar_tensor_tensor(row[:, own], ident[:, :], q_col[:, KB - 1:KB], row[:, own],
                                                     ALU.mult, ALU.add))
            step.settle_apart()
            select(total - 1)
            finish(more * KB + (KB - 2))
            finish(more * KB + (KB - 1), gathered_last, next_best)
            step = Steps(dve, late_step)
            link = step.link
            dve.wait_ge(x1_ready, total)
            link(nc.vector.tensor_scalar(x1_part, x1, 0.9, 1.0, ALU.mult, ALU.add))

            def group(t, g):
                return t[:, g * GB:g * GB + GB, :]

            def spread(col):
                return col.unsqueeze(2).to_broadcast([P, GB, F])

            asked = [0]

            def ask_deviation(h):
                root(measure(asked[0] % 2, [h[:, b, :] for b in range(GB)]))
                asked[0] += 1

            def norm_group(dst, h, signal, count):
                n = (asked[0] - 1) % 2
                wait_root()
                link(nc.vector.reciprocal(rs[:, n, :], sd[:, n, :]))
                for b in range(GB):
                    ins = nc.vector.tensor_scalar(dst[:, b, :], h[:, b, :], moments[:, n, b, 0:1], rs[:, n, b:b + 1],
                                                  ALU.subtract, ALU.mult)
                    if b < GB - 1:
                        step.done(ins)
                ins.then_inc(signal, 1)
                dve.wait_ge(signal, count)

            unscale = 1.0 / (A_SCALE * V_SCALE)

            def acc(layer, g):
                dve.wait_ge(acc_ready, 2 * layer + g // (NG // 2) + 1)
                return banks[[4, 6, 4][layer] + g * GB * F // 512][:, (g * GB * F) % 512:(g * GB * F) % 512 + GB * F] \
                    .rearrange("p (k f) -> p k f", f=F)

            def feature_pair(n, pair, evacuations):
                g = n % NG
                dve.wait_ge(u_evac, evacuations)
                link(nc.vector.tensor_scalar(group(pair[:, :, HI, :], g), group(u_bot, g), V_SCALE, None, ALU.mult))
                nc.vector.scalar_tensor_tensor(group(pair[:, :, LO, :], g), group(u_bot, g), V_SCALE,
                                               group(pair[:, :, HI, :], g), ALU.mult, ALU.subtract) \
                    .then_inc(pair_ready, 1)

            for g in range(NG):
                link(nc.vector.scalar_tensor_tensor(ta, acc(0, g), unscale, group(x1, g), ALU.mult, ALU.mult))
                link(nc.vector.tensor_reduce(red[:, :], ta, AX.X, ALU.add))
                link(nc.vector.scalar_tensor_tensor(ta, spread(red[:, :]), -0.01, group(x1_part, g),
                                                    ALU.mult, ALU.add))
                ask_deviation(ta)
                if g:
                    feature_pair(g - 1, pair2, 2 * g - 1)
                norm_group(group(x2, g), ta, x_ready, g + 1)
            feature_pair(NG - 1, pair2, 2 * NG - 1)

            dve.wait_ge(const_loaded, 96)
            dve.wait_ge(u_evac, 2 * NG)
            for g in range(NG):
                step.done(nc.vector.tensor_tensor(group(z_part, g), group(u_bot, g),
                                                  spread(rdeg[:, g * GB:g * GB + GB]), ALU.mult))
                link(nc.vector.tensor_tensor(group(u_top, g), group(u_top, g),
                                             bias2[:, :].unsqueeze(1).to_broadcast([P, GB, F]), ALU.add))
                link(nc.vector.tensor_tensor(group(z_part, g), group(z_part, g), group(u_top, g), ALU.add))
            dve.wait_ge(pair_ready, NG)
            link(nc.vector.tensor_scalar(rdeg[:, :], rdeg[:, :], unscale, None, ALU.mult))
            for g in range(NG):
                link(nc.vector.tensor_tensor(ta, acc(1, g), spread(rdeg[:, g * GB:g * GB + GB]), ALU.mult))
                link(nc.vector.tensor_tensor(ta, ta, group(z_part, g), ALU.add))
                link(nc.vector.scalar_tensor_tensor(tb, ta, 0.0, ta, ALU.max, ALU.mult))
                root(nc.vector.tensor_reduce(red[:, :], tb, AX.X, ALU.add))
                wait_root()
                link(nc.vector.tensor_scalar(red[:, :], red[:, :], 1e-12, None, ALU.max))
                link(nc.vector.reciprocal(red[:, :], red[:, :]))
                link(nc.vector.scalar_tensor_tensor(tb, ta, 0.0, spread(red[:, :]), ALU.max, ALU.mult))
                link(nc.vector.tensor_tensor(tb, tb, group(x2, g), ALU.add))
                ask_deviation(tb)
                if g:
                    feature_pair(NG + g - 1, pair3, 2 * NG + g)
                norm_group(group(x3, g), tb, x_ready, NG + g + 1)
            feature_pair(2 * NG - 1, pair3, 3 * NG)

            def last_norm(g):
                n = (2 * NG + g) % 2
                dve.wait_ge(root_out, roots[0] - (g + 1 < NG))
                link(nc.vector.reciprocal(rs[:, n, :], sd[:, n, :]))
                nc.vector.scalar_tensor_tensor(shift[:, n, :], moments[:, n, :, 0], -1.0, rs[:, n, :],
                                               ALU.mult, ALU.mult).then_inc(shift_ready, 1)
                for b in range(GB // 2):
                    ins = nc.vector.tensor_scalar(x4[:, g * GB + b, :], [ta, tb][n][:, b, :], moments[:, n, b, 0:1],
                                                  rs[:, n, b:b + 1], ALU.subtract, ALU.mult)
                    if b < GB // 2 - 1:
                        step.done(ins)
                ins.then_inc(out_dve, 1)

            for g in range(NG):
                if g >= 2:
                    dve.wait_ge(out_act, g - 1)
                    dve.wait_ge(out_dve, g - 1)
                h = [ta, tb][(2 * NG + g) % 2]
                link(nc.vector.scalar_tensor_tensor(h, acc(2, g), unscale, group(x3, g), ALU.mult, ALU.add))
                ask_deviation(h)
                if g:
                    last_norm(g - 1)
            last_norm(NG - 1)

        @block.tensor
        def _(pe):
            def features0():
                pe.wait_ge(xw_in_loaded, 32)
                for k in range(KB):
                    ins = nc.tensor.matmul(XW[k // (KB // 2)][:, bass.ts(k % (KB // 2), F)], xT_s[:, bass.ts(k, P)],
                                           w0_s, start=True, stop=True)
                    if k % (KB // 2) == KB // 2 - 1:
                        ins.then_inc(xw_ready, 1)

            def triple(acc, lhs_hi, lhs_lo, rhs_hi, rhs_lo, start, stop, skip=False):
                nc.tensor.matmul(acc, lhs_hi, rhs_hi, start=start, stop=False, skip_group_check=skip)
                nc.tensor.matmul(acc, lhs_hi, rhs_lo, start=False, stop=False, skip_group_check=skip)
                return nc.tensor.matmul(acc, lhs_lo, rhs_hi, start=False, stop=stop, skip_group_check=skip)

            def row_block(r, u):
                for t in range(4):
                    part, h = t // 2, t % 2
                    if h == 0:
                        pe.wait_ge([hi_ready, lo_ready][part], r + 1)
                    if not (isinstance(r, int) and r == 0):
                        pe.wait_ge(tp_evac[t], r)
                    for k in range(KB // 2):
                        ins = nc.tensor.transpose(banks[t][:, :].bitcast(F16)[:, bass.ts(k, P)],
                                                  nat[u][:, part, bass.ts(h * KB // 2 + k, P)], ident16[:, :])
                    ins.then_inc(tp_ready[t], 1)
                    if t == 1:
                        for k in range(KB):
                            nc.tensor.matmul(FLAGS[:, bass.ds(r * KB + k, 1)], nat[u][:, HI, bass.ts(k, P)],
                                             ones16[:, 0:1], start=True, stop=True, skip_group_check=True)

            pe.wait_ge(ident_ready, 1)
            row_block(0, 0)
            row_block(1, 1)
            features0()
            with pe.Fori(1, KB // 2) as pair:
                row_block(pair * 2, 0)
                row_block(pair * 2 + 1, 1)
            nc.tensor.matmul(FLAGS[:, KB * KB:KB * KB + 1], ident16[:, :], ident16[:, 0:1],
                             start=True, stop=True, skip_group_check=True).then_inc(flags_ready, 1)

            def positions():
                pe.wait_ge(tables_ready, 1)
                flags = flags16.rearrange("p (r k) -> p r k", k=KB)
                pos = POS[:, 0:KB * KB].rearrange("p (r k) -> p r k", k=KB)
                nc.tensor.matmul(pos, tri, flags, start=True, stop=False, skip_group_check=True)
                for s in range(1, KB):
                    nc.tensor.matmul(pos[:, :, s:KB], ones16[:, :], flags[:, :, 0:KB - s], start=False,
                                     stop=(s == KB - 1), skip_group_check=True)
                nc.tensor.matmul(COUNTS[:, 0:KB * KB], ones16[:, :], flags16, start=True, stop=True) \
                    .then_inc(pos_ready, 1)

            def list_step(n):
                r, h = n // 2, n % 2
                buf = n % 3
                pe.wait_ge(upper_ready, r + 1)
                if by_act(n):
                    pe.wait_ge(onehot_act, (n + 3) // 4)
                else:
                    pe.wait_ge(onehot_dve, n + 1 - (n + 3) // 4)
                for k in range(HALF):
                    ins = nc.tensor.matmul(LISTS[r // HALF][:, bass.ts(r % HALF, KB)], lower[:, buf, k, :],
                                           upper[:, r % 2, h * HALF + k, :],
                                           start=(h == 0 and k == 0), stop=(h == 1 and k == HALF - 1),
                                           skip_group_check=True)
                ins.then_inc(onehot_used, 1)

            def matvec(n):
                pe.wait_ge(vec_ready, n + 1)
                for i in range(KB):
                    for k in range(KB):
                        nc.tensor.matmul(VEC[:, 2 * i:2 * i + 2], a_block(HI, k, i), vec16[:, k, :],
                                         start=(k == 0), stop=False, skip_group_check=True)
                        nc.tensor.matmul(VEC[:, 2 * i:2 * i + 1], a_block(LO, k, i), vec16[:, k, HI:HI + 1],
                                         start=False, stop=(k == KB - 1), skip_group_check=True)
                    if n == 1 or i >= KB - EARLY:
                        list_step(n * KB + i - (KB - EARLY))
                nc.tensor.matmul(VEC[:, 2 * KB:2 * KB + 1], ident16[:, :], ident16[:, 0:1],
                                 start=True, stop=True).then_inc(mv_ready, 1)

            def spread_g(q):
                pe.wait_ge(gdiag_hi, q + 1)
                pe.wait_ge(gdiag_lo, DIAG * (q + 1))
                nc.tensor.matmul(G_BANKS[q][:, :], ones16[:, :], g_diag[:, q, HI].rearrange("p k c -> p (k c)"),
                                 start=True, stop=False)
                nc.tensor.matmul(G_BANKS[q][:, :], ones16[:, :], g_diag[:, q, LO].rearrange("p k c -> p (k c)"),
                                 start=False, stop=True).then_inc(gbank_ready, 1)

            for t in range(4):
                pe.wait_ge(tp_evac[t], KB)
            positions()
            matvec(0)
            matvec(1)
            for q in range(CH):
                spread_g(q)
            for n in range(KB + EARLY, 2 * KB):
                list_step(n)
            def block_products(lhs_hi, lhs_lo, slot, c, start, stop, n=P):
                cols = bass.ts(c, CW)
                return triple(banks[c][:, :], lhs_hi, lhs_lo, slots[0:n, slot, HI, cols], slots[0:n, slot, LO, cols],
                              start, stop, skip=True)

            more = unit_count(pe)
            units, total = more + 1, more * KB + KB

            def row_of_products(i):
                pe.wait_ge(own_loaded, 16 * i + 16)
                for c in range(CH):
                    pe.wait_ge(tile_evac, units * (i * CH) + (c + 1))
                    ins = block_products(a_block(HI, i, i), a_block(LO, i, i), UNIT, c, True, False)
                ins.then_inc(own_used, 1)
                with pe.Fori(0, units) as g:
                    v = units * i + g
                    for b in range(UNIT):
                        pe.wait_ge(r_loaded[b], v * 16 + 16)
                        pe.wait_ge(listed_ready, v * UNIT + (b + 1))
                        for c in range(CH):
                            if b == 0:
                                pe.wait_ge(tile_evac, v * CH + (c + 1))
                            ins = block_products(listed[0:SLOT, b, HI, :], listed[0:SLOT, b, LO, :], b, c, False,
                                                 b == UNIT - 1, n=SLOT)
                            if b == UNIT - 1:
                                ins.then_inc(tile_ready, 1)
                        if b < UNIT - 1:
                            ins.then_inc(slot_used[b], 1)

            def aggregate(first_bank, pair, ks):
                per = 512 // F
                if ks[-1] < KB - 1:
                    order = [(i, k) for k in ks for i in range(KB)]
                else:
                    order = [(i, k) for i in range(KB) for k in ks]
                for i, k in order:
                    ins = triple(banks[first_bank + i // per][:, bass.ts(i % per, F)], a_block(HI, k, i),
                                 a_block(LO, k, i), pair[:, k, HI, :], pair[:, k, LO, :],
                                 k == 0 and i % per == 0, k == KB - 1, skip=True)
                    if k == KB - 1 and i % per == per - 1:
                        ins.then_inc(acc_ready, 1)

            for i in range(KB + LAG):
                if i < KB:
                    row_of_products(i)
                if i >= LAG:
                    pe.wait_ge(x1_ready, units * (i - LAG + 1))
                    aggregate(4, x1_pair, [i - LAG])

            def project(n, w, width):
                g = n % NG
                src = [x2, x3][n // NG]
                pe.wait_ge(x_ready, n + 1)
                if n >= 2:
                    pe.wait_ge(u_evac, 2 * (n - 1) if n <= NG + 1 else NG + n - 1)
                for b in range(0, GB, 2):
                    ins = nc.tensor.transpose(banks[2 * (n % 2)][:, bass.ts(b // 2, P)],
                                              src[:, g * GB + b:g * GB + b + 2, :].rearrange("p k f -> p (k f)"),
                                              ident[:, :])
                ins.then_inc(xt_ready, 1)
                pe.wait_ge(xt_copied, n + 1)
                for b in range(GB // 2):
                    ins = nc.tensor.matmul(banks[2 * (n % 2) + 1][:, bass.ts(b, 2 * width)],
                                           x_t[n % 2][:, bass.ts(b, P)], w[:, :, :].rearrange("p b f -> p (b f)"),
                                           start=True, stop=True)
                ins.then_inc(u_ready, 1)

            pe.wait_ge(const_loaded, 96)
            for layer, (w, width, pair, first_bank) in enumerate([(w2_s, 2 * F, pair2, 6), (w3_s, F, pair3, 4)]):
                base = layer * NG
                project(base, w, width)
                for g in range(NG):
                    if g + 1 < NG:
                        project(base + g + 1, w, width)
                    pe.wait_ge(pair_ready, base + g + 1)
                    aggregate(first_bank, pair, range(g * GB, g * GB + GB))


def kernel(x, adj, L0_gnn_theta, L0_gnn_W, L0_gnn_b, L1_gnn_t, L2_gnn_W, L2_gnn_b, L3_gnn_weight):
    import numpy as np
    import concourse.bacc as bacc
    from concourse.bass_utils import run_bass_kernel_spmd

    x, adj, w0, w2 = np.asarray(x), np.asarray(adj), np.asarray(L0_gnn_W), np.asarray(L2_gnn_W)
    n, f = x.shape
    kb = n // P
    adjT = np.zeros((kb, n + 1, P), adj.dtype)
    adjT[:, 1:] = adj.reshape(kb, P, n).transpose(0, 2, 1)
    lane, block = np.arange(P), np.arange(kb)
    tables = np.concatenate([
        lane[:, None] < lane[None, :],
        np.broadcast_to(lane, (P, P)),
        np.broadcast_to(np.repeat(block * (n + 1), kb), (P, kb * kb)),
        block[None, :] * P + lane[:, None] + 1,
    ], axis=1).astype(np.float32)
    arrays = {
        "xT": np.ascontiguousarray(x.T),
        "x": x,
        "adj": adj,
        "adjT": adjT.reshape(-1, P),
        "tables": tables,
        "theta": np.asarray(L0_gnn_theta),
        "w0T": np.ascontiguousarray(w0.T),
        "b0": np.asarray(L0_gnn_b),
        "w2": np.ascontiguousarray(np.concatenate([w2[:f], w2[f:]], axis=1)),
        "b2": np.asarray(L2_gnn_b),
        "w3": np.asarray(L3_gnn_weight),
    }
    nc = bacc.Bacc("TRN2", target_bir_lowering=False, num_devices=1)
    args = [nc.dram_tensor(name, a.shape, mybir.dt.from_np(a.dtype), kind="ExternalInput").ap()
            for name, a in arrays.items()]
    xw = nc.dram_tensor("xw", (n, f), F32, kind="Internal").ap()
    r_pairs = nc.dram_tensor("r_pairs", (n, 2 * n), F16, kind="Internal").ap()
    out = nc.dram_tensor("out", (n, f), F32, kind="ExternalOutput").ap()
    graph_layers(nc, *args, xw, r_pairs, out)
    r = run_bass_kernel_spmd(nc, [arrays], core_ids=[0])
    return r.results[0]["out"]
```
